# Optimizing a Trainium2 kernel written in Bass

```python
import numpy as np
import jax
import jax.numpy as jnp

def _softmax(x, axis=-1):
    return jax.nn.softmax(x, axis=axis)

def _gelu(x):
    return jax.nn.gelu(x, approximate=True)

def _silu(x):
    return jax.nn.silu(x)

def _sigmoid(x):
    return jax.nn.sigmoid(x)

def _layernorm(x, axis=-1, eps=1e-05):
    m = jnp.mean(x, axis=axis, keepdims=True)
    v = jnp.var(x, axis=axis, keepdims=True)
    return (x - m) / jnp.sqrt(v + eps)

def _scatter_add(tgt, idx, src, axis=0):
    return tgt.at[idx].add(src)

def _segment_sum(src, seg, n):
    return jax.ops.segment_sum(src, seg, n)
kernel_name = 'mk_lm_tower_d2_tok_ids512_r4_d7c9fa'

def setup_inputs(seed: int=0):
    np.random.seed(seed)
    _w = jnp.asarray

    def _rec_inputs():
        import jax
        import jax.numpy as jnp
        _rk = jax.random.key(seed)
        x = jax.random.randint(jax.random.fold_in(_rk, 1), (8, 512), 0, 31993, jnp.int32)
        return x
    x = _rec_inputs()

    def _L0_tok_setup():
        import jax, jax.numpy as jnp
        import numpy as np
        VOCAB = 8000
        EMBED = 128
        key = jax.random.key(seed)
        k_idx, k_w, k_b = jax.random.split(key, 3)
        input_indices = jax.random.randint(k_idx, (4, 512), 0, VOCAB, dtype=jnp.int64)
        fan_in = VOCAB
        bound = 1.0 / np.sqrt(fan_in)
        W = jax.random.uniform(k_w, (EMBED, VOCAB), jnp.float32, -bound, bound)
        b = jax.random.uniform(k_b, (EMBED,), jnp.float32, -bound, bound)
        return {'input_indices': input_indices, 'W': W, 'b': b}
    _L0_tok_all = _L0_tok_setup()
    _L0_tok_in = {k: v for k, v in _L0_tok_all.items() if k in ('W', 'b')}
    del _L0_tok_all

    def _L0_attn_setup():
        import math
        import jax, jax.numpy as jnp
        import numpy as np
        D_MODEL = 128
        N_HEADS = 8
        D_K = D_MODEL // N_HEADS
        LN_EPS = 1e-05

        def _rel_pos_encoding(length: int, d: int) -> jnp.ndarray:
            pos = jnp.arange(length, dtype=jnp.float32)[:, None]
            div = jnp.exp(jnp.arange(0, d, 2, dtype=jnp.float32) * -(math.log(10000.0) / d))
            ang = pos * div[None, :]
            return jnp.stack([jnp.sin(ang), jnp.cos(ang)], axis=-1).reshape(length, d)
        key = jax.random.key(seed)
        ks = jax.random.split(key, 6)
        B, T = (4, 512)
        s = 1.0 / math.sqrt(D_MODEL)
        return {'x': jax.random.normal(ks[0], (B, T, D_MODEL), dtype=jnp.float32), 'ln_g': jnp.ones((D_MODEL,), jnp.float32), 'ln_b': jnp.zeros((D_MODEL,), jnp.float32), 'wq': jax.random.normal(ks[1], (D_MODEL, D_MODEL), jnp.float32) * s, 'bq': jnp.zeros((D_MODEL,), jnp.float32), 'wk': jax.random.normal(ks[2], (D_MODEL, D_MODEL), jnp.float32) * s, 'bk': jnp.zeros((D_MODEL,), jnp.float32), 'wv': jax.random.normal(ks[3], (D_MODEL, D_MODEL), jnp.float32) * s, 'bv': jnp.zeros((D_MODEL,), jnp.float32), 'wo': jax.random.normal(ks[4], (D_MODEL, D_MODEL), jnp.float32) * s, 'bo': jnp.zeros((D_MODEL,), jnp.float32)}
    _L0_attn_all = _L0_attn_setup()
    _L0_attn_in = {k: v for k, v in _L0_attn_all.items() if k in ('ln_g', 'ln_b', 'wq', 'bq', 'wk', 'bk', 'wv', 'bv', 'wo', 'bo')}
    del _L0_attn_all

    def _L0_ffn_setup():
        import jax, jax.numpy as jnp
        import numpy as np
        DIM = 128
        HID = 384
        N_EXPERTS = 8
        TOP_K = 2
        SHARED_HID = HID * 2
        B, S = (4, 512)

        def _swiglu(x, w1, w3, w2):
            return jax.nn.silu(x @ w1.T) * (x @ w3.T) @ w2.T
        key = jax.random.key(seed)
        ks = jax.random.split(key, 8)
        sc_d = 1.0 / np.sqrt(DIM)
        sc_h = 1.0 / np.sqrt(HID)
        sc_sh = 1.0 / np.sqrt(SHARED_HID)
        return {'x': jax.random.normal(ks[0], (B, S, DIM), jnp.float32), 'gate_w': jax.random.normal(ks[1], (N_EXPERTS, DIM), jnp.float32) * sc_d, 'w1': jax.random.normal(ks[2], (N_EXPERTS, HID, DIM), jnp.float32) * sc_d, 'w3': jax.random.normal(ks[3], (N_EXPERTS, HID, DIM), jnp.float32) * sc_d, 'w2': jax.random.normal(ks[4], (N_EXPERTS, DIM, HID), jnp.float32) * sc_h, 'sw1': jax.random.normal(ks[5], (SHARED_HID, DIM), jnp.float32) * sc_d, 'sw3': jax.random.normal(ks[6], (SHARED_HID, DIM), jnp.float32) * sc_d, 'sw2': jax.random.normal(ks[7], (DIM, SHARED_HID), jnp.float32) * sc_sh}
    _L0_ffn_all = _L0_ffn_setup()
    _L0_ffn_in = {k: v for k, v in _L0_ffn_all.items() if k in ('gate_w', 'w1', 'w3', 'w2', 'sw1', 'sw3', 'sw2')}
    del _L0_ffn_all

    def _L1_attn_setup():
        import jax, jax.numpy as jnp
        import numpy as np
        DIM = 128
        HEADS = 8
        HEAD_DIM = DIM // HEADS
        EPS = 1e-05

        def bqe(x, mu):
            cs = x.shape[-1] // 4
            x_star = jnp.concatenate([x[..., :cs], jnp.roll(x[..., cs:2 * cs], 1, axis=1), jnp.roll(x[..., 2 * cs:3 * cs], -1, axis=1), jnp.roll(x[..., 3 * cs:], 2, axis=1)], axis=-1)
            return x + (1.0 - jax.nn.sigmoid(mu)) * x_star

        def wkv_scan(r, k, v, w, u):
            B, H, T, D = r.shape
            rT, kT, vT, wT = (jnp.moveaxis(a, 2, 0) for a in (r, k, v, w))

            def step(state, inp):
                rt, kt, vt, wt = inp
                state_contrib = jnp.einsum('bhde,bhe->bhd', state, kt)
                bonus = kt * u[None] * vt.sum(-1, keepdims=True)
                ot = jax.nn.sigmoid(rt) * (state_contrib + bonus)
                new_state = wt[..., None] * state + kt[..., None] * vt[..., None, :]
                return (new_state, ot)
            state0 = jnp.zeros((B, H, D, D), r.dtype)
            _, out = jax.lax.scan(step, state0, (rT, kT, vT, wT))
            return jnp.moveaxis(out, 0, 2)

        def wkv_attention(x, mu_r, mu_k, mu_v, mu_w, Wr, Wk, Wv, Wg, Ww, decay_A, decay_B, decay_base, u, gn_w, gn_b, Wout):
            B, T, C = x.shape
            H, D = (HEADS, HEAD_DIM)
            r = bqe(x, mu_r) @ Wr.T
            k = bqe(x, mu_k) @ Wk.T
            v = bqe(x, mu_v) @ Wv.T
            g = jax.nn.sigmoid(x @ Wg.T)
            c = bqe(x, mu_w) @ Ww.T
            w = jnp.exp(-jnp.exp(decay_base + jnp.tanh(c * decay_A) * decay_B))

            def heads(a):
                return a.reshape(B, T, H, D).transpose(0, 2, 1, 3)
            r, k, v, w = (heads(r), heads(k), heads(v), heads(w))
            wkv_fwd = wkv_scan(r, k, v, w, u)
            flip = lambda a: jnp.flip(a, axis=2)
            wkv_bwd = flip(wkv_scan(flip(r), flip(k), flip(v), flip(w), u))
            wkv = 0.5 * (wkv_fwd + wkv_bwd)
            o = wkv.transpose(0, 2, 1, 3)
            mean = o.mean(axis=(1, 3), keepdims=True)
            var = o.var(axis=(1, 3), keepdims=True)
            o = (o - mean) * jax.lax.rsqrt(var + EPS)
            o = o * gn_w.reshape(1, 1, H, D) + gn_b.reshape(1, 1, H, D)
            out = o.reshape(B, T, C) * g
            return out @ Wout.T
        key = jax.random.key(seed)
        ks = jax.random.split(key, 12)
        wmat = lambda k: jax.random.normal(k, (DIM, DIM), jnp.float32) * 0.02
        return {'x': jax.random.normal(ks[0], (16, 1024, DIM), jnp.float32), 'mu_r': jnp.zeros(DIM, jnp.float32), 'mu_k': jnp.zeros(DIM, jnp.float32), 'mu_v': jnp.zeros(DIM, jnp.float32), 'mu_w': jnp.zeros(DIM, jnp.float32), 'Wr': wmat(ks[1]), 'Wk': wmat(ks[2]), 'Wv': wmat(ks[3]), 'Wg': wmat(ks[4]), 'Ww': wmat(ks[5]), 'decay_A': jax.random.normal(ks[6], (DIM,), jnp.float32) * 0.01, 'decay_B': jax.random.normal(ks[7], (DIM,), jnp.float32) * 0.01, 'decay_base': jax.random.normal(ks[8], (DIM,), jnp.float32) * 0.01, 'u': jax.random.normal(ks[9], (HEADS, HEAD_DIM), jnp.float32) * 0.01, 'gn_w': jnp.ones(DIM, jnp.float32), 'gn_b': jnp.zeros(DIM, jnp.float32), 'Wout': wmat(ks[10])}
    _L1_attn_all = _L1_attn_setup()
    _L1_attn_in = {k: v for k, v in _L1_attn_all.items() if k in ('mu_r', 'mu_k', 'mu_v', 'mu_w', 'Wr', 'Wk', 'Wv', 'Wg', 'Ww', 'decay_A', 'decay_B', 'decay_base', 'u', 'gn_w', 'gn_b', 'Wout')}
    del _L1_attn_all

    def _L1_ffn_setup():
        import jax, jax.numpy as jnp
        import numpy as np
        B, T, D = (4, 2048, 128)
        E, F, CAP = (8, 512, 1024)
        key = jax.random.key(seed)
        ks = jax.random.split(key, 6)
        s = 0.02
        return {'x': jax.random.normal(ks[0], (B, T, D), dtype=jnp.float32), 'Wr': jax.random.normal(ks[1], (D, E), dtype=jnp.float32) * s, 'W1': jax.random.normal(ks[2], (E, D, F), dtype=jnp.float32) * s, 'b1': jax.random.normal(ks[3], (E, F), dtype=jnp.float32) * s, 'W2': jax.random.normal(ks[4], (E, F, D), dtype=jnp.float32) * s, 'b2': jax.random.normal(ks[5], (E, D), dtype=jnp.float32) * s}
    _L1_ffn_all = _L1_ffn_setup()
    _L1_ffn_in = {k: v for k, v in _L1_ffn_all.items() if k in ('Wr', 'W1', 'b1', 'W2', 'b2')}
    del _L1_ffn_all
    return {'x': x, 'L0_tok_W': _L0_tok_in['W'], 'L0_tok_b': _L0_tok_in['b'], 'L0_attn_ln_g': _L0_attn_in['ln_g'], 'L0_attn_ln_b': _L0_attn_in['ln_b'], 'L0_attn_wq': _L0_attn_in['wq'], 'L0_attn_bq': _L0_attn_in['bq'], 'L0_attn_wk': _L0_attn_in['wk'], 'L0_attn_bk': _L0_attn_in['bk'], 'L0_attn_wv': _L0_attn_in['wv'], 'L0_attn_bv': _L0_attn_in['bv'], 'L0_attn_wo': _L0_attn_in['wo'], 'L0_attn_bo': _L0_attn_in['bo'], 'L0_ffn_gate_w': _L0_ffn_in['gate_w'], 'L0_ffn_w1': _L0_ffn_in['w1'], 'L0_ffn_w3': _L0_ffn_in['w3'], 'L0_ffn_w2': _L0_ffn_in['w2'], 'L0_ffn_sw1': _L0_ffn_in['sw1'], 'L0_ffn_sw3': _L0_ffn_in['sw3'], 'L0_ffn_sw2': _L0_ffn_in['sw2'], 'L1_attn_mu_r': _L1_attn_in['mu_r'], 'L1_attn_mu_k': _L1_attn_in['mu_k'], 'L1_attn_mu_v': _L1_attn_in['mu_v'], 'L1_attn_mu_w': _L1_attn_in['mu_w'], 'L1_attn_Wr': _L1_attn_in['Wr'], 'L1_attn_Wk': _L1_attn_in['Wk'], 'L1_attn_Wv': _L1_attn_in['Wv'], 'L1_attn_Wg': _L1_attn_in['Wg'], 'L1_attn_Ww': _L1_attn_in['Ww'], 'L1_attn_decay_A': _L1_attn_in['decay_A'], 'L1_attn_decay_B': _L1_attn_in['decay_B'], 'L1_attn_decay_base': _L1_attn_in['decay_base'], 'L1_attn_u': _L1_attn_in['u'], 'L1_attn_gn_w': _L1_attn_in['gn_w'], 'L1_attn_gn_b': _L1_attn_in['gn_b'], 'L1_attn_Wout': _L1_attn_in['Wout'], 'L1_ffn_Wr': _L1_ffn_in['Wr'], 'L1_ffn_W1': _L1_ffn_in['W1'], 'L1_ffn_b1': _L1_ffn_in['b1'], 'L1_ffn_W2': _L1_ffn_in['W2'], 'L1_ffn_b2': _L1_ffn_in['b2']}

def reference(x, L0_tok_W, L0_tok_b, L0_attn_ln_g, L0_attn_ln_b, L0_attn_wq, L0_attn_bq, L0_attn_wk, L0_attn_bk, L0_attn_wv, L0_attn_bv, L0_attn_wo, L0_attn_bo, L0_ffn_gate_w, L0_ffn_w1, L0_ffn_w3, L0_ffn_w2, L0_ffn_sw1, L0_ffn_sw3, L0_ffn_sw2, L1_attn_mu_r, L1_attn_mu_k, L1_attn_mu_v, L1_attn_mu_w, L1_attn_Wr, L1_attn_Wk, L1_attn_Wv, L1_attn_Wg, L1_attn_Ww, L1_attn_decay_A, L1_attn_decay_B, L1_attn_decay_base, L1_attn_u, L1_attn_gn_w, L1_attn_gn_b, L1_attn_Wout, L1_ffn_Wr, L1_ffn_W1, L1_ffn_b1, L1_ffn_W2, L1_ffn_b2):
    import jax
    import jax.numpy as jnp

    def _L0_tok_ref(input_indices, W, b):
        import jax, jax.numpy as jnp
        import numpy as np
        VOCAB = 8000
        EMBED = 128
        B, S = input_indices.shape
        one_hot = jax.nn.one_hot(input_indices, VOCAB, dtype=jnp.float32)
        embedding = jnp.einsum('bsv,ev->bse', one_hot, W) + b
        return embedding

    def _L0_attn_ref(x, ln_g, ln_b, wq, bq, wk, bk, wv, bv, wo, bo):
        import math
        import jax, jax.numpy as jnp
        import numpy as np
        D_MODEL = 128
        N_HEADS = 8
        D_K = D_MODEL // N_HEADS
        LN_EPS = 1e-05

        def _rel_pos_encoding(length: int, d: int) -> jnp.ndarray:
            pos = jnp.arange(length, dtype=jnp.float32)[:, None]
            div = jnp.exp(jnp.arange(0, d, 2, dtype=jnp.float32) * -(math.log(10000.0) / d))
            ang = pos * div[None, :]
            return jnp.stack([jnp.sin(ang), jnp.cos(ang)], axis=-1).reshape(length, d)
        B, T, D = x.shape
        mu = jnp.mean(x, axis=-1, keepdims=True)
        var = jnp.mean(jnp.square(x - mu), axis=-1, keepdims=True)
        normed = (x - mu) * jax.lax.rsqrt(var + LN_EPS) * ln_g + ln_b

        def split_heads(y):
            return y.reshape(B, T, N_HEADS, D_K).transpose(0, 2, 1, 3)
        Q = split_heads(normed @ wq.T + bq)
        K = split_heads(normed @ wk.T + bk)
        V = split_heads(normed @ wv.T + bv)
        pe = _rel_pos_encoding(T, D_K)
        K = K + pe[None, None, :, :]
        scale = 1.0 / math.sqrt(D_K)
        scores = jnp.einsum('bhtd,bhsd->bhts', Q, K) * scale
        attn = jax.nn.softmax(scores, axis=-1)
        context = jnp.einsum('bhts,bhsd->bhtd', attn, V)
        context = context.transpose(0, 2, 1, 3).reshape(B, T, D)
        return context @ wo.T + bo

    def _L0_ffn_ref(x, gate_w, w1, w3, w2, sw1, sw3, sw2):
        import jax, jax.numpy as jnp
        import numpy as np
        DIM = 128
        HID = 384
        N_EXPERTS = 8
        TOP_K = 2
        SHARED_HID = HID * 2
        B, S = (4, 512)

        def _swiglu(x, w1, w3, w2):
            return jax.nn.silu(x @ w1.T) * (x @ w3.T) @ w2.T
        b, s, d = x.shape
        t = b * s
        xf = x.reshape(t, d)
        logits = xf.astype(jnp.float32) @ gate_w.astype(jnp.float32).T
        scores = jax.nn.softmax(logits, axis=-1)
        topk_w, topk_i = jax.lax.top_k(scores, TOP_K)
        e = gate_w.shape[0]
        comb = jnp.zeros((t, e), jnp.float32).at[jnp.arange(t)[:, None], topk_i].add(topk_w)
        y = jnp.zeros((t, d), x.dtype)
        for i in range(e):
            ye = _swiglu(xf, w1[i], w3[i], w2[i]).astype(x.dtype)
            y = y + comb[:, i:i + 1].astype(x.dtype) * ye
        y = y.reshape(b, s, d)
        shared = _swiglu(xf, sw1, sw3, sw2).reshape(b, s, d).astype(x.dtype)
        return y + shared

    def _L1_attn_ref(x, mu_r, mu_k, mu_v, mu_w, Wr, Wk, Wv, Wg, Ww, decay_A, decay_B, decay_base, u, gn_w, gn_b, Wout):
        import jax, jax.numpy as jnp
        import numpy as np
        DIM = 128
        HEADS = 8
        HEAD_DIM = DIM // HEADS
        EPS = 1e-05

        def bqe(x, mu):
            cs = x.shape[-1] // 4
            x_star = jnp.concatenate([x[..., :cs], jnp.roll(x[..., cs:2 * cs], 1, axis=1), jnp.roll(x[..., 2 * cs:3 * cs], -1, axis=1), jnp.roll(x[..., 3 * cs:], 2, axis=1)], axis=-1)
            return x + (1.0 - jax.nn.sigmoid(mu)) * x_star

        def wkv_scan(r, k, v, w, u):
            B, H, T, D = r.shape
            rT, kT, vT, wT = (jnp.moveaxis(a, 2, 0) for a in (r, k, v, w))

            def step(state, inp):
                rt, kt, vt, wt = inp
                state_contrib = jnp.einsum('bhde,bhe->bhd', state, kt)
                bonus = kt * u[None] * vt.sum(-1, keepdims=True)
                ot = jax.nn.sigmoid(rt) * (state_contrib + bonus)
                new_state = wt[..., None] * state + kt[..., None] * vt[..., None, :]
                return (new_state, ot)
            state0 = jnp.zeros((B, H, D, D), r.dtype)
            _, out = jax.lax.scan(step, state0, (rT, kT, vT, wT))
            return jnp.moveaxis(out, 0, 2)

        def wkv_attention(x, mu_r, mu_k, mu_v, mu_w, Wr, Wk, Wv, Wg, Ww, decay_A, decay_B, decay_base, u, gn_w, gn_b, Wout):
            B, T, C = x.shape
            H, D = (HEADS, HEAD_DIM)
            r = bqe(x, mu_r) @ Wr.T
            k = bqe(x, mu_k) @ Wk.T
            v = bqe(x, mu_v) @ Wv.T
            g = jax.nn.sigmoid(x @ Wg.T)
            c = bqe(x, mu_w) @ Ww.T
            w = jnp.exp(-jnp.exp(decay_base + jnp.tanh(c * decay_A) * decay_B))

            def heads(a):
                return a.reshape(B, T, H, D).transpose(0, 2, 1, 3)
            r, k, v, w = (heads(r), heads(k), heads(v), heads(w))
            wkv_fwd = wkv_scan(r, k, v, w, u)
            flip = lambda a: jnp.flip(a, axis=2)
            wkv_bwd = flip(wkv_scan(flip(r), flip(k), flip(v), flip(w), u))
            wkv = 0.5 * (wkv_fwd + wkv_bwd)
            o = wkv.transpose(0, 2, 1, 3)
            mean = o.mean(axis=(1, 3), keepdims=True)
            var = o.var(axis=(1, 3), keepdims=True)
            o = (o - mean) * jax.lax.rsqrt(var + EPS)
            o = o * gn_w.reshape(1, 1, H, D) + gn_b.reshape(1, 1, H, D)
            out = o.reshape(B, T, C) * g
            return out @ Wout.T
        return wkv_attention(x, mu_r, mu_k, mu_v, mu_w, Wr, Wk, Wv, Wg, Ww, decay_A, decay_B, decay_base, u, gn_w, gn_b, Wout)

    def _L1_ffn_ref(x, Wr, W1, b1, W2, b2):
        import jax, jax.numpy as jnp
        import numpy as np
        B, T, D = (4, 2048, 128)
        E, F, CAP = (8, 512, 1024)
        Bb, Tt, Dd = x.shape
        N = Bb * Tt
        C = min(CAP, N)
        x_flat = x.reshape(N, Dd)
        logits = x_flat @ Wr
        probs = jax.nn.softmax(logits, axis=0)
        vals, idx = jax.lax.top_k(probs.T, C)
        selected = x_flat[idx]
        h = jax.nn.gelu(jnp.einsum('ecd,edf->ecf', selected, W1) + b1[:, None, :], approximate=False)
        out_e = jnp.einsum('ecf,efd->ecd', h, W2) + b2[:, None, :]
        weighted = vals[..., None] * out_e
        output = jnp.zeros_like(x_flat).at[idx.reshape(-1)].add(weighted.reshape(-1, Dd))
        return output.reshape(Bb, Tt, Dd)
    h = _L0_tok_ref(x, L0_tok_W, L0_tok_b)
    h = h + _L0_attn_ref(_layernorm(h, axis=-1), L0_attn_ln_g, L0_attn_ln_b, L0_attn_wq, L0_attn_bq, L0_attn_wk, L0_attn_bk, L0_attn_wv, L0_attn_bv, L0_attn_wo, L0_attn_bo)
    h = h + _L0_ffn_ref(_layernorm(h, axis=-1), L0_ffn_gate_w, L0_ffn_w1, L0_ffn_w3, L0_ffn_w2, L0_ffn_sw1, L0_ffn_sw3, L0_ffn_sw2)
    h = h + _L1_attn_ref(_layernorm(h, axis=-1), L1_attn_mu_r, L1_attn_mu_k, L1_attn_mu_v, L1_attn_mu_w, L1_attn_Wr, L1_attn_Wk, L1_attn_Wv, L1_attn_Wg, L1_attn_Ww, L1_attn_decay_A, L1_attn_decay_B, L1_attn_decay_base, L1_attn_u, L1_attn_gn_w, L1_attn_gn_b, L1_attn_Wout)
    h = h + _L1_ffn_ref(_layernorm(h, axis=-1), L1_ffn_Wr, L1_ffn_W1, L1_ffn_b1, L1_ffn_W2, L1_ffn_b2)
    return h

_drawn_inputs = setup_inputs


def setup_inputs(seed=0):
    import zlib

    import numpy as np

    out = dict(_drawn_inputs(seed))
    spreads = {'L0_attn_ln_g': (1.0, 0.2),
     'L0_attn_ln_b': (0.0, 0.1),
     'L0_attn_bq': (0.0, 0.8),
     'L0_attn_bk': (0.0, 2.0),
     'L0_attn_bv': (0.0, 0.1),
     'L0_attn_bo': (0.0, 0.1),
     'L1_attn_mu_r': (0.0, 2.0),
     'L1_attn_mu_k': (0.0, 0.8),
     'L1_attn_mu_v': (0.0, 2.0),
     'L1_attn_mu_w': (0.0, 2.0),
     'L1_attn_gn_w': (1.0, 0.6),
     'L1_attn_gn_b': (0.0, 0.8)}
    factors = {'L1_attn_Wr': 3.658,
     'L1_attn_Wg': 5.416,
     'L1_attn_Ww': 64.0,
     'L1_attn_decay_A': 64.0,
     'L1_attn_decay_B': 64.0,
     'L1_attn_decay_base': 64.0,
     'L1_attn_u': 8.0,
     'L1_ffn_Wr': 64.0,
     'L1_ffn_W1': 64.0,
     'L1_ffn_b1': 64.0,
     'L1_ffn_W2': 64.0,
     'L1_ffn_b2': 64.0}
    for name, (base, spread) in spreads.items():
        noise = np.random.default_rng([zlib.crc32(name.encode()), seed]).standard_normal(out[name].shape)
        drawn = base * np.exp(spread * noise) if base else spread * noise
        out[name] = jnp.asarray(drawn.astype(out[name].dtype))
    for name, factor in factors.items():
        out[name] = (out[name] * factor).astype(out[name].dtype)
    return out
```

```python
import concourse.bass as bass
from concourse import mybir
from contextlib import ExitStack


class Chain:

    def __init__(self, eng, sem):
        self.eng, self.sem, self.base, self.n = eng, sem, 0, 0

    def step(self, ins):
        ins.then_inc(self.sem, 1)
        self.n += 1

    def wait(self, apart=None):
        self.eng.wait_ge(self.sem, self.base + self.n)
        if apart is not None:
            self.eng.nop().then_inc(apart, 1)

    def link(self, ins, apart=None):
        self.step(ins)
        self.wait(apart)

    def enter(self, i, per):
        self.start, self.per = self.base + self.n, per
        self.base, self.n = self.start + i * per, 0

    def leave(self, turns):
        assert self.n == self.per, f"{self.n} steps a turn, not {self.per}"
        self.base, self.n = self.start + turns * self.per, 0


def lm_tower(nc, t, out, upto=3):
    fp32, f32r, i32 = mybir.dt.float32, mybir.dt.float32r, mybir.dt.int32
    ALU, ACT, AX = mybir.AluOpType, mybir.ActivationFunctionType, mybir.AxisListType.X
    ds = bass.ds

    P = 128
    B, T, D = 8, 512, 128
    NT = B * T // P
    TQ = T // P
    NH, DK = 8, 16
    VOCAB = t["emb"].shape[0]
    EPS = 1e-5
    NE, HID, TOPK = 8, 384, 2
    HT = HID // P
    FT = t["f1"].shape[2] // P
    CAP = 1024
    CAP = min(CAP, B * T)
    SHT = t["sw1"].shape[1] // P
    SCALE = DK ** -0.5
    GH = 4
    NG = NH // GH

    ctx = ExitStack()
    with ctx:
        space = ctx

        def sb(name, shape, dt=fp32):
            return space.enter_context(nc.sbuf_tensor(name, shape, dt))

        def sem(name):
            return ctx.enter_context(nc.semaphore(name))

        bank = ctx.enter_context(nc.psum_tensor("bank", [P, 8, 512], fp32))

        h = sb("h", [P, NT, D])
        ident = sb("ident", [P, P])
        ident_r = sb("ident_r", [P, P], f32r)
        ones_row = sb("ones_row", [1, 512])
        half_neg = sb("half_neg", [P, NT])
        token_id = sb("token_id", [P, NT], i32)
        tok_b = sb("tok_b", [P, D])
        stats = sb("stats", [P, NT, 6])
        mv = sb("mv", [P, NT, 2])
        var_eps = sb("var_eps", [P, NT])
        rstd = sb("rstd", [P, NT])
        rstd2 = sb("rstd2", [P, NT])
        y = sb("y", [P, TQ, D])
        yT = sb("yT", [P, T])

        gate_w = sb("gate_w", [P, NE])
        w1, w3 = sb("w1", [P, NE, HID]), sb("w3", [P, NE, HID])
        w2 = sb("w2", [P, NE, HT, D])
        sw1, sw3, sw2 = sb("sw1", [P, SHT * P]), sb("sw3", [P, SHT * P]), sb("sw2", [P, SHT, D])
        tri = sb("tri", [P, NE, NE])
        top = sb("top", [P, TQ])
        score = sb("score", [P, TQ, NE])
        better = sb("better", [P, TQ, NE, NE])
        tied = sb("tied", [P, TQ, NE, NE])
        comb = sb("comb", [P, TQ, NE])
        gated = sb("gated", [P, 2, T])
        act = sb("act", [P, 2, SHT, T])
        acc = sb("acc", [P, TQ, D])

        lent = ExitStack()
        space = lent
        vec = sb("vec", [P, 8])
        wq, wk, wv = sb("wq", [P, D]), sb("wk", [P, D]), sb("wv", [P, NG * P])
        wo = sb("wo", [P, NG, D])
        bo_row = sb("bo_row", [1, D])
        bv_pad = sb("bv_pad", [P, NG * P])
        pe = sb("pe", [P, T])
        spread_f = sb("spread_f", [P, 4, 4 * P])
        spread = sb("spread", [P, 4, 4 * P], f32r)
        pick_sum = sb("pick_sum", [P, GH])
        part = sb("part", [P, 4, T], f32r)
        k_full = sb("k_full", [P, T])
        q_rows = sb("q_rows", [P, 4, T], f32r)
        qm_rows = sb("qm_rows", [P, 4, T], f32r)
        k_rows = sb("k_rows", [P, 4, T], f32r)
        v_tok = sb("v_tok", [P, TQ, NG * P])
        neg_max = sb("neg_max", [P, NG, TQ, GH])
        max_cols = sb("max_cols", [P, 4, TQ, P], f32r)
        probs = sb("probs", [P, 4, 2, T])
        ctx_raw = sb("ctx_raw", [P, NG, T])
        ctx_n = sb("ctx_n", [P, NG, T])
        recip = sb("recip", [P, TQ * GH])
        recip_cols = sb("recip_cols", [P, TQ, P])

        lent.close()
        space = ctx

        mix_w = sb("mix_w", [P, 5, D])
        wout = sb("wout", [P, D])
        vec1 = sb("vec1", [P, 10])
        keep_mu = sb("keep_mu", [P, 4])
        pick = sb("pick", [P, DK, P], f32r)
        pick_f = act[:, 0, 0:4, :].rearrange("p k n -> p (k n)")
        head_ones = sb("head_ones", [P, P])
        head_ones_r = sb("head_ones_r", [P, P], f32r)

        router = sb("router", [P, NE])
        f1 = sb("f1", [P, NE, FT * P])
        f2 = sb("f2", [P, NE, FT, D])
        fb1 = sb("fb1", [P, NE * FT])
        fb2_row = sb("fb2_row", [1, NE * D])
        bits = sb("bits", [P, 30], i32)
        same_e, before = sb("same_e", [P, P]), sb("before", [P, P])

        lent = ExitStack()
        space = lent
        x_star = sb("x_star", [P, T])
        mixed = sb("mixed", [P, 4, T])
        k1 = sb("k1", [P, T])
        part1 = sb("part1", [P, 4, T], f32r)
        decay = sb("decay", [P, T])
        sig_r, sig_g = sb("sig_r", [P, T]), sb("sig_g", [P, T])
        bonus = sb("bonus", [P, T])
        v_all = sb("v_all", [P, 2, T])
        kv = sb("kv", [P, 2, T])
        fwd, bwd = sb("fwd", [P, 2, T + 1]), sb("bwd", [P, 2, T + 1])
        both = sb("both", [P, 2, T])
        term = sb("term", [P, 2, T])
        wkv = sb("wkv", [P, T])
        gn_stat, gn_mv = sb("gn_stat", [P, 6]), sb("gn_mv", [P, 2])
        gn_mean, gn_dev, gn_var = sb("gn_mean", [P, 1]), sb("gn_dev", [P, 1]), sb("gn_var", [P, 1])
        gn_rstd, gn_gain, gn_off = sb("gn_rstd", [P, 1]), sb("gn_gain", [P, 1]), sb("gn_off", [P, 1])

        lent.close()
        space = ctx

        yT_all = sb("yT_all", [P, B * T])
        lg = sb("lg", [NE, B * T])
        lg_top, lg_sum = sb("lg_top", [NE, 1]), sb("lg_sum", [NE, 1])
        NC = P // NE
        CW = B * T // NC
        prob = sb("prob", [P, CW])
        thr, cand, keep = sb("thr", [P, 1], i32), sb("cand", [P, 1], i32), sb("keep", [P, 1], i32)
        hit, rank, ones_cw = sb("hit", [P, CW]), sb("rank", [P, CW]), sb("ones_cw", [P, CW])
        count, need = sb("count", [P, 1]), sb("need", [P, 1])
        chosen = sb("chosen", [P, CW])
        comb1 = sb("comb1", [P, 2 * P])

        s_const = sem("s_const")
        s_weights0 = sem("s_weights0")
        s_setup = sem("s_setup")
        s_emb = [sem(f"s_emb{b}") for b in range(B)]
        s_apart, s_apart_act, s_apart_pool = sem("s_apart"), sem("s_apart_act"), sem("s_apart_pool")
        s_dve, s_act, s_pool = sem("s_dve"), sem("s_act"), sem("s_pool")
        s_out = sem("s_out")
        s_phase = [sem(f"s_phase{n}") for n in range(6)]

        s_var, s_rstd = sem("s_var"), sem("s_rstd")
        s_y, s_yt, s_ytc = sem("s_y"), sem("s_yt"), sem("s_ytc")
        s_qkv, s_split, s_v = sem("s_qkv"), sem("s_split"), sem("s_v")
        s_rep, s_repc = sem("s_rep"), sem("s_repc")
        s_s1, s_max, s_m = sem("s_s1"), sem("s_max"), sem("s_m")
        s_mrow, s_qm = sem("s_mrow"), sem("s_qm")
        s_s2, s_exp, s_av = sem("s_s2"), sem("s_exp"), sem("s_av")
        s_ctx, s_sum, s_rec, s_bc, s_cn = sem("s_ctx"), sem("s_sum"), sem("s_rec"), sem("s_bc"), sem("s_cn")
        s_o = sem("s_o")

        s_bvar, s_brstd = sem("s_bvar"), sem("s_brstd")
        s_by, s_byt, s_bytc = sem("s_by"), sem("s_byt"), sem("s_bytc")
        s_logit, s_logc, s_escore = sem("s_logit"), sem("s_logc"), sem("s_escore")
        s_gu, s_silu, s_actv, s_ye, s_yec = sem("s_gu"), sem("s_silu"), sem("s_actv"), sem("s_ye"), sem("s_yec")

        s_cvar, s_crstd = sem("s_cvar"), sem("s_crstd")
        s_cy, s_cyt, s_cytc, s_star = sem("s_cy"), sem("s_cyt"), sem("s_cytc"), sem("s_star")
        s_mix, s_proj, s_kv_split = sem("s_mix"), sem("s_proj"), sem("s_kv_split")
        s_mu, s_w, s_sig, s_vsum = sem("s_mu"), sem("s_w"), sem("s_sig"), sem("s_vsum")
        s_vb, s_vbc, s_kv, s_kb = sem("s_vb"), sem("s_vbc"), sem("s_kv"), sem("s_kb")
        s_scan, s_both, s_term, s_acc = sem("s_scan"), sem("s_both"), sem("s_term"), sem("s_acc")
        s_gm, s_gmr, s_gvar, s_grstd, s_on, s_co = (sem("s_gm"), sem("s_gmr"), sem("s_gvar"), sem("s_grstd"),
                                                    sem("s_on"), sem("s_co"))
        s_weights1, s_weights2 = sem("s_weights1"), sem("s_weights2")

        s_dvar, s_drstd = sem("s_dvar"), sem("s_drstd")
        s_dy, s_dyt, s_dytc, s_dcopy = sem("s_dy"), sem("s_dyt"), sem("s_dytc"), sem("s_dcopy")
        s_dl, s_dlc = sem("s_dl"), sem("s_dlc")
        s_ltop, s_lexp, s_lprob, s_spread = sem("s_ltop"), sem("s_lexp"), sem("s_lprob"), sem("s_spread")
        s_cnt, s_tot, s_pw, s_pwt, s_comb1 = sem("s_cnt"), sem("s_tot"), sem("s_pw"), sem("s_pwt"), sem("s_comb1")
        s_up, s_gelu, s_fo, s_foc = sem("s_up"), sem("s_gelu"), sem("s_fo"), sem("s_foc")

        WEIGHTS1 = [(pick_f, t["pick"]), (mix_w[:, :, :], t["mix_w"].rearrange("m c d -> c m d")), (wout[:, :], t["wout"]),
                    (vec1[:, :], t["vec1"]), (head_ones[:, :], t["head_ones"])]
        WEIGHTS2 = [(router[:, :], t["router"]), (f1[:, :, :], t["f1"].rearrange("e d f -> d e f")),
                    (f2[:, :, :, :], t["f2"].rearrange("e (k p) d -> p e k d", p=P)),
                    (fb1[:, :], t["fb1"]), (fb2_row[:, :], t["fb2"]), (bits[:, :], t["bits"]),
                    (same_e[:, :], t["head_ones"]), (before[:, :], t["before"])]
        CONSTS = [(vec[:, :], t["vec"]), (ident[:, :], t["ident"]), (wq[:, :], t["wq"]), (wk[:, :], t["wk"]),
                  (wv[:, :], t["wv"]), (wo[:, :, :], t["wo"].rearrange("g p n -> p g n")),
                  (bo_row[:, :], t["bo"]), (bv_pad[:, :], t["bv"].partition_broadcast(P)),
                  (pe[:, :], t["pe"]), (spread_f[:, :, :], t["spread"]), (pick_sum[:, :], t["pick_sum"]),
                  (tok_b[:, :], t["tok_b"].partition_broadcast(P)), (token_id[:, :], t["x"])]
        WEIGHTS0 = [(gate_w[:, :], t["gate_w"]), (w1[:, :, :], t["w1"].rearrange("e d f -> d e f")),
                    (w3[:, :, :], t["w3"].rearrange("e d f -> d e f")),
                    (w2[:, :, :, :], t["w2"].rearrange("e (k p) d -> p e k d", p=P)),
                    (sw1[:, :], t["sw1"]), (sw3[:, :], t["sw3"]),
                    (sw2[:, :, :], t["sw2"].rearrange("(k p) d -> p k d", p=P)),
                    (tri[:, :, :], t["tri"].partition_broadcast(P))]
        consts_in = (s_const, 16 * len(CONSTS))

        def phase_end(eng, n):
            eng.nop().then_inc(s_phase[n], 1)
            eng.wait_ge(s_phase[n], 4)

        def maxima(p, hh):
            return 64 * hh + 3 * DK

        NU1, NU2 = NG * GH * TQ, NG * TQ * 2
        EARLY = 4

        block = ctx.enter_context(nc.Block())

        @block.sync
        def _(sp):
            for dst, src in CONSTS:
                sp.dma_start(dst, src).then_inc(s_const, 16)
            for dst, src in WEIGHTS0:
                sp.dma_start(dst, src).then_inc(s_weights0, 16)
            sp.wait_ge(s_phase[0], 4)
            for dst, src in WEIGHTS1[1:]:
                sp.dma_start(dst, src).then_inc(s_weights1, 16)
            for dst, src in WEIGHTS2:
                sp.dma_start(dst, src).then_inc(s_weights2, 16)
            sp.wait_ge(s_phase[1], 4)
            sp.dma_start(*WEIGHTS1[0]).then_inc(s_weights1, 16)
            if upto >= 3:
                sp.wait_ge(s_lprob, 1)
                sp.dma_start(prob[:, :], lg[:, :].rearrange("e (c n) -> e c n", c=NC)).then_inc(s_spread, 16)
            sp.wait_ge(s_phase[5 if upto == 3 else upto], 4)
            sp.dma_start(out.rearrange("b (j p) d -> p (b j) d", p=P), h[:, :, :]).then_inc(s_out, 16)
            sp.wait_ge(s_out, 16)

        @block.gpsimd
        def _(pool):
            pool.memset(h[:, :, :], 0.0).then_inc(s_pool, 1)
            pool.memset(half_neg[:, :], -0.5).then_inc(s_pool, 1)
            pool.wait_ge(s_pool, 2)
            pool.wait_ge(*consts_in)
            for j in range(NT):
                pool.indirect_dma_start(
                    out=h[:, j, :], out_offset=None, in_=t["emb"],
                    in_offset=bass.IndirectOffsetOnAxis(ap=token_id[:, j:j + 1], axis=0),
                    bounds_check=VOCAB - 1, oob_is_err=False).then_inc(s_emb[j // TQ], 16)

            pool.wait_ge(s_var, 1)
            pool.tensor_tensor(rstd[:, :], var_eps[:, :], half_neg[:, :], ALU.pow).then_inc(s_rstd, 1)
            pool.wait_ge(s_var, 2)
            pool.tensor_tensor(rstd2[:, :], var_eps[:, :], half_neg[:, :], ALU.pow).then_inc(s_rstd, 1)
            phase_end(pool, 0)
            if upto < 1:
                return

            with pool.Fori(0, B) as b:
                pool.wait_ge(s_bvar, b + 1)
                pool.tensor_tensor(rstd[:, 0:TQ], var_eps[:, 0:TQ], half_neg[:, 0:TQ], ALU.pow).then_inc(s_brstd, 1)
            phase_end(pool, 1)
            if upto < 2:
                return

            with pool.Fori(0, B) as b:
                pool.wait_ge(s_cvar, b + 1)
                pool.tensor_tensor(rstd[:, 0:TQ], var_eps[:, 0:TQ], half_neg[:, 0:TQ], ALU.pow).then_inc(s_crstd, 1)

                def add_directions(e):
                    pool.wait_ge(s_scan, DK * b + e + 1)
                    if e >= 2:
                        pool.wait_ge(s_term, DK * b + e - 1)
                    pool.tensor_tensor(both[:, e % 2, :], fwd[:, e % 2, 0:T], bwd[:, e % 2, 1:T + 1],
                                       ALU.add).then_inc(s_both, 1)

                for e in range(DK):
                    pool.wait_ge(s_vbc, DK * b + e + 1)
                    if e == 0:
                        pool.wait_ge(s_kv_split, 3 * b + 1)
                    if e >= 2:
                        pool.wait_ge(s_scan, DK * b + e - 1)
                    pool.tensor_tensor(kv[:, e % 2, :], k1[:, :], v_all[:, e % 2, :], ALU.mult).then_inc(s_kv, 1)
                    if e:
                        add_directions(e - 1)
                add_directions(DK - 1)
                pool.wait_ge(s_gvar, b + 1)
                pool.tensor_tensor(gn_rstd[:, :], gn_var[:, :], half_neg[:, 0:1], ALU.pow).then_inc(s_grstd, 1)
            phase_end(pool, 2)
            if upto < 3:
                return

            with pool.Fori(0, B) as b:
                pool.wait_ge(s_dvar, b + 1)
                pool.tensor_tensor(rstd[:, 0:TQ], var_eps[:, 0:TQ], half_neg[:, 0:TQ], ALU.pow).then_inc(s_drstd, 1)
                pool.wait_ge(s_dytc, b + 1)
                pool.nop().then_inc(s_apart_pool, 1)
                pool.tensor_copy(yT_all[:, ds(b * T, T)], yT[:, :]).then_inc(s_dcopy, 1)
            phase_end(pool, 3)
            phase_end(pool, 4)
            phase_end(pool, 5)

        @block.scalar
        def _(act_e):
            act_e.wait_ge(*consts_in)
            ch = Chain(act_e, s_act)
            with act_e.Fori(0, B) as b:
                act_e.wait_ge(s_yt, b + 1)
                nc.scalar.activation(yT[:, :], bank[:, 0, :], ACT.Identity, bias=vec[:, 1:2],
                                     scale=vec[:, 0:1]).then_inc(s_ytc, 1)
                for n in range(8):
                    p, to_k = n // 2, n % 2
                    act_e.wait_ge(s_rep, 8 * b + n + 1)
                    if to_k:
                        nc.scalar.activation(k_rows[:, p, :], bank[:, n % 2, :], ACT.Identity,
                                             bias=vec[:, 4:5]).then_inc(s_repc, 1)
                    else:
                        nc.scalar.activation(q_rows[:, p, :], bank[:, n % 2, :], ACT.Copy).then_inc(s_repc, 1)
                for u in range(NU2):
                    g, kt = u // 8, (u % 8) // 2
                    a = u // 2
                    act_e.wait_ge(s_s2, NU2 * b + u + 1)
                    if a >= 2:
                        act_e.wait_ge(s_av, 8 * b + a - 1)
                    s = 4 + 2 * (u % 2)
                    nc.scalar.activation(probs[:, u % 4, :, :], bank[:, s:s + 2, :], ACT.Exp,
                                         scale=SCALE).then_inc(s_exp, 1)
                    if u % 8 == 7:
                        act_e.wait_ge(s_av, 8 * b + 4 * g + 4)
                        nc.scalar.activation(ctx_raw[:, g, :], bank[:, 1, :], ACT.Copy).then_inc(s_ctx, 1)
            phase_end(act_e, 0)
            if upto < 1:
                return

            act_e.wait_ge(s_weights0, 16 * len(WEIGHTS0))
            NX = 3 * NE + SHT
            with act_e.Fori(0, B) as b:
                act_e.wait_ge(s_byt, b + 1)
                nc.scalar.activation(yT[:, :], bank[:, 0, :], ACT.Copy).then_inc(s_bytc, 1)
                act_e.wait_ge(s_logc, b + 1)
                nc.scalar.activation(score[:, :, :], score[:, :, :], ACT.Exp).then_inc(s_escore, 1)
                for n in range(NX):
                    act_e.wait_ge(s_gu, NX * b + n + 1)
                    if n >= 2:
                        act_e.wait_ge(s_actv, NX * b + n - 1)
                    nc.scalar.activation(gated[:, n % 2, :], bank[:, 2 + 2 * (n % 2), :],
                                         ACT.Silu).then_inc(s_silu, 1)
            phase_end(act_e, 1)
            if upto < 2:
                return

            act_e.wait_ge(s_weights1, 16 * len(WEIGHTS1))
            nc.scalar.activation(keep_mu[:, :], vec1[:, 0:4], ACT.Sigmoid).then_inc(s_mu, 1)
            with act_e.Fori(0, B) as b:
                act_e.wait_ge(s_cyt, b + 1)
                nc.scalar.activation(yT[:, :], bank[:, 0, :], ACT.Copy).then_inc(s_cytc, 1)
                act_e.wait_ge(s_cytc, b + 1)
                for s, shift in enumerate((0, 1, -1, 2)):
                    r = slice(32 * s, 32 * s + 32)
                    for o, i, n in ((max(shift, 0), max(-shift, 0), T - abs(shift)),
                                    (0 if shift > 0 else T + shift, T - shift if shift > 0 else 0, abs(shift))):
                        if n:
                            last = nc.scalar.activation(x_star[r, o:o + n], yT[r, i:i + n], ACT.Copy)
                last.then_inc(s_star, 1)
                act_e.wait_ge(s_proj, 5 * b + 1)
                nc.scalar.activation(decay[:, :], bank[:, 4, :], ACT.Tanh, scale=vec1[:, 4:5]).then_inc(s_w, 1)
                act_e.wait_ge(s_w, 3 * b + 1)
                nc.scalar.activation(decay[:, :], decay[:, :], ACT.Exp, scale=vec1[:, 5:6],
                                     bias=vec1[:, 6:7]).then_inc(s_w, 1)
                act_e.wait_ge(s_w, 3 * b + 2)
                nc.scalar.activation(decay[:, :], decay[:, :], ACT.Exp, scale=-1.0).then_inc(s_w, 1)
                act_e.wait_ge(s_proj, 5 * b + 4)
                nc.scalar.activation(sig_r[:, :], bank[:, 1, :], ACT.Sigmoid).then_inc(s_sig, 1)
                act_e.wait_ge(s_proj, 5 * b + 5)
                nc.scalar.activation(sig_g[:, :], bank[:, 5, :], ACT.Sigmoid).then_inc(s_sig, 1)
                for e in range(DK):
                    act_e.wait_ge(s_vb, DK * b + e + 1)
                    if e >= 2:
                        act_e.wait_ge(s_kv, DK * b + e - 1)
                    nc.scalar.activation(v_all[:, e % 2, :], bank[:, 1 + e % 2, :], ACT.Copy).then_inc(s_vbc, 1)
            phase_end(act_e, 2)
            if upto < 3:
                return

            with act_e.Fori(0, B) as b:
                act_e.wait_ge(s_dyt, b + 1)
                nc.scalar.activation(yT[:, :], bank[:, 0, :], ACT.Copy).then_inc(s_dytc, 1)
                act_e.wait_ge(s_dl, b + 1)
                act_e.nop().then_inc(s_apart_act, 1)
                nc.scalar.activation(lg[:, ds(b * T, T)], bank[0:NE, 1, :], ACT.Copy).then_inc(s_dlc, 1)
            phase_end(act_e, 3)
            act_e.wait_ge(s_ltop, 1)
            nc.scalar.activation(lg[:, :], lg[:, :], ACT.Exp, bias=lg_top[:, :],
                                 accum_out=lg_sum[:, :]).then_inc(s_lexp, 1)
            phase_end(act_e, 4)
            with act_e.Fori(0, B) as b:
                for n in range(NE * FT):
                    x, k = n // FT, n % FT
                    act_e.wait_ge(s_up, NE * FT * b + n + 1)
                    if k == 0 and x >= 2:
                        act_e.wait_ge(s_fo, NE * b + x - 1)
                    nc.scalar.activation(act[:, x % 2, k, :], bank[:, 2 + n % 4, :], ACT.Gelu,
                                         bias=fb1[:, n:n + 1]).then_inc(s_gelu, 1)
            phase_end(act_e, 5)

        @block.vector
        def _(dve):
            ch = Chain(dve, s_dve)
            v = nc.vector
            dve.wait_ge(*consts_in)
            v.tensor_copy(ident_r[:, :], ident[:, :]).then_inc(s_setup, 1)
            v.tensor_copy(spread[:, :, :], spread_f[:, :, :]).then_inc(s_setup, 1)
            v.memset(ones_row[:, :], 1.0).then_inc(s_setup, 1)
            v.memset(max_cols[:, :, :, :].bitcast(fp32), 0.0).then_inc(s_setup, 1)
            for b in range(B):
                dve.wait_ge(s_emb[b], 16 * TQ)
                hb = h[:, TQ * b:TQ * (b + 1), :]
                ch.link(v.tensor_tensor(hb, hb, tok_b[:, None, :].broadcast_to([P, TQ, D]), ALU.add))
                for j in range(TQ * b, TQ * (b + 1)):
                    ch.step(v.bn_stats(stats[:, j, :], h[:, j, :]))
            ch.wait()
            for j in range(NT):
                ch.step(v.bn_aggr(mv[:, j, :], stats[:, j, :]))
            ch.wait()
            v.tensor_scalar(var_eps[:, :], mv[:, :, 1], EPS, None, ALU.add).then_inc(s_var, 1)
            dve.wait_ge(s_rstd, 1)
            ch.link(v.tensor_tensor(var_eps[:, :], rstd[:, :], rstd[:, :], ALU.mult))
            ch.link(v.tensor_tensor(var_eps[:, :], var_eps[:, :], mv[:, :, 1], ALU.mult))
            ch.step(v.tensor_scalar(var_eps[:, :], var_eps[:, :], EPS, None, ALU.add))
            ch.wait()
            dve.nop().then_inc(s_var, 1)
            dve.wait_ge(s_rstd, 2)
            ch.link(v.tensor_tensor(rstd[:, :], rstd[:, :], rstd2[:, :], ALU.mult))

            with dve.Fori(0, B) as b:
                ch.enter(b, 2 + 1 + 2 * 1 + 2 * 2 + 1)
                for j in range(TQ):
                    last = v.tensor_scalar(y[:, j, :], h[:, ds(b * TQ + j, 1), :].rearrange("p a d -> p (a d)"),
                                           mv[:, ds(b * TQ + j, 1), 0], rstd[:, ds(b * TQ + j, 1)],
                                           ALU.subtract, ALU.mult)
                last.then_inc(s_y, 1)
                dve.wait_ge(s_qkv, 3 * b + 1)
                ch.link(v.tensor_scalar(part[:, 0, :], bank[:, 4, :], vec[:, 2:3], None, ALU.add))
                v.scalar_tensor_tensor(part[:, 1, :], bank[:, 4, :], vec[:, 2:3], part[:, 0, :].bitcast(fp32),
                                       ALU.add, ALU.subtract).then_inc(s_split, 1)
                dve.wait_ge(s_qkv, 3 * b + 2)
                ch.link(v.scalar_tensor_tensor(k_full[:, :], bank[:, 5, :], vec[:, 3:4], pe[:, :],
                                               ALU.add, ALU.add))
                ch.link(v.tensor_copy(part[:, 2, :], k_full[:, :]))
                v.tensor_tensor(part[:, 3, :], k_full[:, :], part[:, 2, :].bitcast(fp32),
                                ALU.subtract).then_inc(s_split, 1)
                dve.wait_ge(s_qkv, 3 * b + 3)
                v.tensor_tensor(v_tok[:, :, :], bank[:, 6:8, :].rearrange("p k (c n) -> p (k c) n", c=2),
                                bv_pad[:, None, :].broadcast_to([P, TQ, NG * P]), ALU.add).then_inc(s_v, 1)

                def maxes(g, ns):
                    for n in ns:
                        h4, qt = n // TQ, n % TQ
                        m = g * GH * TQ + n
                        dve.wait_ge(s_s1, NU1 * b + m + 1)
                        v.tensor_reduce(neg_max[:, g, qt, h4:h4 + 1], bank[:, 2 + m % 2, :], AX, ALU.max,
                                        negate=True).then_inc(s_max, 1)

                def max_parts(g):
                    dve.wait_ge(s_max, NU1 * b + GH * TQ * (g + 1))
                    hi = [max_cols[:, 2 * g + pp, :, :].rearrange("p q (a c) -> p q a c", a=2)[:, :, :, 3 * DK]
                          for pp in range(2)]
                    lo = [max_cols[:, 2 * g + pp, :, :].rearrange("p q (a c) -> p q a c", a=2)[:, :, :, 3 * DK + 1]
                          for pp in range(2)]
                    for pp in range(2):
                        last = v.tensor_copy(hi[pp], neg_max[:, g, :, 2 * pp:2 * pp + 2])
                    ch.link(last)
                    for pp in range(2):
                        last = v.tensor_tensor(lo[pp], neg_max[:, g, :, 2 * pp:2 * pp + 2], hi[pp].bitcast(fp32),
                                               ALU.subtract)
                    last.then_inc(s_m, 1)

                def add_max_rows(g):
                    for pp in range(2):
                        n = 2 * g + pp
                        dve.wait_ge(s_mrow, 4 * b + n + 1)
                        v.tensor_tensor(qm_rows[:, n, :], q_rows[:, n, :].bitcast(fp32), bank[:, 0, :],
                                        ALU.add).then_inc(s_qm, 1)

                def divide(g):
                    dve.wait_ge(s_sum, 2 * b + g + 1)
                    ch.link(v.reciprocal(recip[:, :], bank[:, 0, g * TQ * GH:(g + 1) * TQ * GH]))
                    v.tensor_copy(recip_cols[:, :, :].rearrange("p q (a c) -> p (q a) c", a=GH),
                                  recip[:, :, None].broadcast_to([P, TQ * GH, 32])).then_inc(s_rec, 1)
                    dve.wait_ge(s_bc, 2 * b + g + 1)
                    ch.step(v.tensor_tensor(ctx_n[:, g, :], ctx_raw[:, g, :], bank[:, 2, :], ALU.mult))
                    ch.wait()
                    dve.nop().then_inc(s_cn, 1)

                maxes(0, range(GH * TQ))
                max_parts(0)
                maxes(1, range(EARLY))
                add_max_rows(0)
                maxes(1, range(EARLY, GH * TQ))
                max_parts(1)
                add_max_rows(1)
                divide(0)
                divide(1)
                dve.wait_ge(s_o, b + 1)
                hb = h[:, ds(b * TQ, TQ), :]
                ch.link(v.tensor_tensor(hb, hb, bank[:, 0, :].rearrange("p (q d) -> p q d", q=TQ), ALU.add))
            ch.leave(B)
            phase_end(dve, 0)
            if upto < 1:
                return

            NX = 3 * NE + SHT
            dve.wait_ge(s_weights0, 16 * len(WEIGHTS0))
            with dve.Fori(0, B) as b:
                ch.enter(b, 2 + 10 + NE + 1)
                for j in range(TQ):
                    last = v.bn_stats(stats[:, j, :], h[:, ds(b * TQ + j, 1), :].rearrange("p a d -> p (a d)"))
                ch.link(last, apart=s_apart)
                for j in range(TQ):
                    last = v.bn_aggr(mv[:, j, :], stats[:, j, :])
                ch.link(last)
                v.tensor_scalar(var_eps[:, 0:TQ], mv[:, 0:TQ, 1], EPS, None, ALU.add).then_inc(s_bvar, 1)
                dve.wait_ge(s_brstd, b + 1)
                for j in range(TQ):
                    last = v.tensor_scalar(y[:, j, :], h[:, ds(b * TQ + j, 1), :].rearrange("p a d -> p (a d)"),
                                           mv[:, j, 0:1], rstd[:, j:j + 1], ALU.subtract, ALU.mult)
                last.then_inc(s_by, 1)
                dve.wait_ge(s_logit, b + 1)
                logit = bank[:, 1, 0:TQ * NE].rearrange("p (q e) -> p q e", e=NE)
                ch.link(v.tensor_reduce(top[:, :], logit, AX, ALU.max))
                v.tensor_tensor(score[:, :, :], logit, top[:, :, None].broadcast_to([P, TQ, NE]),
                                ALU.subtract).then_inc(s_logc, 1)
                dve.wait_ge(s_escore, b + 1)
                ch.link(v.tensor_reduce(top[:, :], score[:, :, :], AX, ALU.add))
                ch.link(v.reciprocal(top[:, :], top[:, :]))
                ch.link(v.tensor_tensor(score[:, :, :], score[:, :, :],
                                        top[:, :, None].broadcast_to([P, TQ, NE]), ALU.mult))
                for q in range(TQ):
                    other = score[:, q, None, :].broadcast_to([P, NE, NE])
                    own = score[:, q, :, None].broadcast_to([P, NE, NE])
                    v.tensor_tensor(better[:, q, :, :], other, own, ALU.is_gt)
                    last = v.tensor_tensor(tied[:, q, :, :], other, own, ALU.is_equal)
                ch.link(last)
                for q in range(TQ):
                    last = v.tensor_tensor(tied[:, q, :, :], tied[:, q, :, :], tri[:, :, :], ALU.mult)
                ch.link(last)
                ch.link(v.tensor_tensor(better[:, :, :, :].rearrange("p q e f -> p (q e f)"),
                                        better[:, :, :, :].rearrange("p q e f -> p (q e f)"),
                                        tied[:, :, :, :].rearrange("p q e f -> p (q e f)"), ALU.add))
                ch.link(v.tensor_reduce(comb[:, :, :], better[:, :, :, :], AX, ALU.add))
                ch.link(v.tensor_scalar(comb[:, :, :], comb[:, :, :], float(TOPK), None, ALU.is_lt))
                ch.link(v.tensor_tensor(comb[:, :, :], comb[:, :, :], score[:, :, :], ALU.mult))
                n = 0
                for x in range(NE + 1):
                    for k in range(HT if x < NE else SHT):
                        dve.wait_ge(s_silu, NX * b + n + 1)
                        if k == 0 and x >= 2:
                            dve.wait_ge(s_ye, (NE + 1) * b + x - 1)
                        v.tensor_tensor(act[:, x % 2, k, :], gated[:, n % 2, :], bank[:, 3 + 2 * (n % 2), :],
                                        ALU.mult).then_inc(s_actv, 1)
                        n += 1
                    dve.wait_ge(s_ye, (NE + 1) * b + x + 1)
                    ye = bank[:, 6 + x % 2, :].rearrange("p (q d) -> p q d", q=TQ)
                    if x == NE:
                        ch.step(v.tensor_tensor(h[:, ds(b * TQ, TQ), :], ye, acc[:, :, :], ALU.add))
                        ch.wait()
                        dve.nop().then_inc(s_yec, 1)
                        continue
                    for q in range(TQ):
                        onto = acc[:, q, :] if x else h[:, ds(b * TQ + q, 1), :].rearrange("p a d -> p (a d)")
                        last = v.scalar_tensor_tensor(acc[:, q, :], ye[:, q, :], comb[:, q, x:x + 1], onto,
                                                      ALU.mult, ALU.add)
                    ch.link(last)
                    dve.nop().then_inc(s_yec, 1)
            ch.leave(B)
            phase_end(dve, 1)
            if upto < 2:
                return

            dve.wait_ge(s_weights1, 16 * len(WEIGHTS1))
            dve.wait_ge(s_mu, 1)
            v.tensor_scalar(keep_mu[:, :], keep_mu[:, :], -1.0, 1.0, ALU.mult, ALU.add).then_inc(s_setup, 1)
            v.tensor_copy(pick[:, :, :].rearrange("p e n -> p (e n)"), pick_f).then_inc(s_setup, 1)
            v.tensor_copy(head_ones_r[:, :], head_ones[:, :]).then_inc(s_setup, 1)
            v.memset(fwd[:, :, 0:1], 0.0).then_inc(s_setup, 1)
            v.memset(bwd[:, :, T:T + 1], 0.0).then_inc(s_setup, 1)
            dve.wait_ge(s_setup, 9)
            with dve.Fori(0, B) as b:
                ch.enter(b, 2 + 3 + 3 + 7 + 1)
                for j in range(TQ):
                    last = v.bn_stats(stats[:, j, :], h[:, ds(b * TQ + j, 1), :].rearrange("p a d -> p (a d)"))
                ch.link(last, apart=s_apart)
                for j in range(TQ):
                    last = v.bn_aggr(mv[:, j, :], stats[:, j, :])
                ch.link(last)
                v.tensor_scalar(var_eps[:, 0:TQ], mv[:, 0:TQ, 1], EPS, None, ALU.add).then_inc(s_cvar, 1)
                dve.wait_ge(s_crstd, b + 1)
                for j in range(TQ):
                    last = v.tensor_scalar(y[:, j, :], h[:, ds(b * TQ + j, 1), :].rearrange("p a d -> p (a d)"),
                                           mv[:, j, 0:1], rstd[:, j:j + 1], ALU.subtract, ALU.mult)
                last.then_inc(s_cy, 1)
                dve.wait_ge(s_star, b + 1)
                for m in (3, 1, 2, 0):
                    v.scalar_tensor_tensor(mixed[:, m, :], x_star[:, :], keep_mu[:, m:m + 1], yT[:, :],
                                           ALU.mult, ALU.add).then_inc(s_mix, 1)
                dve.wait_ge(s_proj, 5 * b + 2)
                v.tensor_copy(k1[:, :], bank[:, 2, :]).then_inc(s_kv_split, 1)
                ch.link(v.tensor_copy(part1[:, 0, :], bank[:, 2, :]))
                v.tensor_tensor(part1[:, 1, :], bank[:, 2, :], part1[:, 0, :].bitcast(fp32),
                                ALU.subtract).then_inc(s_kv_split, 1)
                dve.wait_ge(s_proj, 5 * b + 3)
                ch.link(v.tensor_copy(part1[:, 2, :], bank[:, 3, :]))
                v.tensor_tensor(part1[:, 3, :], bank[:, 3, :], part1[:, 2, :].bitcast(fp32),
                                ALU.subtract).then_inc(s_kv_split, 1)
                dve.wait_ge(s_vsum, b + 1)
                ch.link(v.scalar_tensor_tensor(bonus[:, :], k1[:, :], vec1[:, 7:8], bank[:, 6, :],
                                               ALU.mult, ALU.mult))
                dve.wait_ge(s_w, 3 * b + 3)

                def terms(e):
                    dve.wait_ge(s_both, DK * b + e + 1)
                    dve.wait_ge(s_kb, DK * b + e + 1)
                    if e >= 2:
                        dve.wait_ge(s_acc, DK * b + e - 1)
                    v.tensor_tensor(term[:, e % 2, :], both[:, e % 2, :], bank[:, 3 + e % 2, :],
                                    ALU.mult).then_inc(s_term, 1)

                for e in range(DK):
                    dve.wait_ge(s_kv, DK * b + e + 1)
                    if e >= 2:
                        dve.wait_ge(s_both, DK * b + e - 1)
                    v.tensor_tensor_scan(fwd[:, e % 2, 1:T + 1], decay[:, :], kv[:, e % 2, :], 0.0,
                                         ALU.mult, ALU.add)
                    v.tensor_tensor_scan(bwd[:, e % 2, 0:T][:, ::-1], decay[:, ::-1], kv[:, e % 2, ::-1], 0.0,
                                         ALU.mult, ALU.add).then_inc(s_scan, 1)
                    if e:
                        terms(e - 1)
                terms(DK - 1)
                dve.wait_ge(s_acc, DK * b + DK)
                ch.link(v.scalar_tensor_tensor(wkv[:, :], bank[:, 7, :], 0.5, bonus[:, :], ALU.mult, ALU.add))
                dve.wait_ge(s_sig, 2 * b + 1)
                ch.link(v.tensor_tensor(wkv[:, :], wkv[:, :], sig_r[:, :], ALU.mult))
                ch.link(v.bn_stats(gn_stat[:, :], wkv[:, :]), apart=s_apart)
                v.bn_aggr(gn_mv[:, :], gn_stat[:, :]).then_inc(s_gm, 1)
                dve.wait_ge(s_gmr, 2 * b + 1)
                dve.wait_ge(s_gm, 2 * b + 1)
                ch.link(v.tensor_scalar(gn_mean[:, :], bank[:, 5, 0:1], 1.0 / DK, None, ALU.mult))
                ch.link(v.tensor_tensor(gn_dev[:, :], gn_mv[:, 0:1], gn_mean[:, :], ALU.subtract))
                ch.link(v.tensor_tensor(gn_dev[:, :], gn_dev[:, :], gn_dev[:, :], ALU.mult))
                v.tensor_tensor(gn_dev[:, :], gn_dev[:, :], gn_mv[:, 1:2], ALU.add).then_inc(s_gm, 1)
                dve.wait_ge(s_gmr, 2 * b + 2)
                v.tensor_scalar(gn_var[:, :], bank[:, 5, 2:3], 1.0 / DK, EPS, ALU.mult, ALU.add).then_inc(s_gvar, 1)
                dve.wait_ge(s_grstd, b + 1)
                ch.link(v.tensor_tensor(gn_gain[:, :], gn_rstd[:, :], vec1[:, 8:9], ALU.mult))
                ch.link(v.tensor_tensor(gn_off[:, :], gn_gain[:, :], gn_mean[:, :], ALU.mult))
                ch.link(v.tensor_tensor(gn_off[:, :], vec1[:, 9:10], gn_off[:, :], ALU.subtract))
                dve.wait_ge(s_sig, 2 * b + 2)
                ch.link(v.tensor_scalar(wkv[:, :], wkv[:, :], gn_gain[:, :], gn_off[:, :], ALU.mult, ALU.add))
                v.tensor_tensor(wkv[:, :], wkv[:, :], sig_g[:, :], ALU.mult).then_inc(s_on, 1)
                dve.wait_ge(s_co, b + 1)
                hb = h[:, ds(b * TQ, TQ), :]
                ch.link(v.tensor_tensor(hb, hb, bank[:, 0, :].rearrange("p (q d) -> p q d", q=TQ), ALU.add))
            ch.leave(B)
            phase_end(dve, 2)
            if upto < 3:
                return

            dve.nop().then_inc(s_foc, 2)
            v.memset(ones_cw[:, :], 1.0).then_inc(s_setup, 1)
            v.memset(thr[:, :], 0).then_inc(s_setup, 1)
            with dve.Fori(0, B) as b:
                ch.enter(b, 2)
                for j in range(TQ):
                    last = v.bn_stats(stats[:, j, :], h[:, ds(b * TQ + j, 1), :].rearrange("p a d -> p (a d)"))
                ch.link(last, apart=s_apart)
                for j in range(TQ):
                    last = v.bn_aggr(mv[:, j, :], stats[:, j, :])
                ch.link(last)
                v.tensor_scalar(var_eps[:, 0:TQ], mv[:, 0:TQ, 1], EPS, None, ALU.add).then_inc(s_dvar, 1)
                dve.wait_ge(s_drstd, b + 1)
                if True:
                    for j in range(TQ):
                        last = v.tensor_scalar(y[:, j, :], h[:, ds(b * TQ + j, 1), :].rearrange("p a d -> p (a d)"),
                                               mv[:, j, 0:1], rstd[:, j:j + 1], ALU.subtract, ALU.mult)
                last.then_inc(s_dy, 1)
                dve.wait_ge(s_dyt, b + 1)
                dve.nop()
            ch.leave(B)
            phase_end(dve, 3)
            ch.link(v.tensor_reduce(lg_top[:, :], lg[:, :], AX, ALU.max, negate=True))
            dve.nop().then_inc(s_ltop, 1)
            dve.wait_ge(s_lexp, 1)
            ch.link(v.reciprocal(lg_sum[:, :], lg_sum[:, :]))
            v.tensor_scalar(lg[:, :], lg[:, :], lg_sum[:, :], None, ALU.mult).then_inc(s_lprob, 1)
            dve.wait_ge(s_spread, 16)
            dve.wait_ge(s_weights2, 16 * len(WEIGHTS2))
            dve.wait_ge(s_setup, 11)
            with dve.Fori(0, 30) as i:
                ch.enter(i, 3)
                ch.link(v.tensor_tensor(cand[:, :], thr[:, :], bits[:, ds(i, 1)], ALU.bitwise_or))
                v.tensor_scalar(hit[:, :], prob[:, :], cand[:, :].bitcast(fp32), None, ALU.is_ge, ALU.add,
                                accum_out=count[:, :]).then_inc(s_cnt, 1)
                dve.wait_ge(s_tot, i + 1)
                dve.wait_ge(s_cnt, i + 1)
                ch.link(v.tensor_scalar(keep[:, :], bank[:, 0, 0:1], float(CAP), None, ALU.is_ge), apart=s_apart)
                ch.link(v.copy_predicated(thr[:, :], keep[:, :], cand[:, :]))
            ch.leave(30)
            thr_f = thr[:, :].bitcast(fp32)
            ch.step(v.tensor_scalar(chosen[:, :], prob[:, :], thr_f, None, ALU.is_gt, ALU.add,
                                    accum_out=count[:, :]))
            ch.wait()
            dve.nop().then_inc(s_cnt, 1)
            dve.wait_ge(s_tot, 31)
            ch.link(v.tensor_scalar(need[:, :], bank[:, 0, 1:2], -1.0, float(CAP), ALU.mult, ALU.add))
            ch.link(v.tensor_scalar(hit[:, :], prob[:, :], thr_f, None, ALU.is_equal))
            ch.link(v.tensor_tensor_scan(rank[:, :], ones_cw[:, :], hit[:, :], 0.0, ALU.mult, ALU.add))
            ch.step(v.tensor_copy(count[:, :], rank[:, CW - 1:CW]))
            ch.wait()
            dve.nop().then_inc(s_cnt, 1)
            dve.wait_ge(s_tot, 32)
            ch.link(v.tensor_tensor(rank[:, :], rank[:, :], hit[:, :], ALU.subtract))
            ch.link(v.tensor_scalar(rank[:, :], rank[:, :], bank[:, 0, 2:3], need[:, :], ALU.add, ALU.is_lt))
            ch.link(v.tensor_tensor(hit[:, :], hit[:, :], rank[:, :], ALU.mult))
            ch.link(v.tensor_tensor(chosen[:, :], chosen[:, :], hit[:, :], ALU.add))
            v.tensor_tensor(chosen[:, :], chosen[:, :], prob[:, :], ALU.mult).then_inc(s_pw, 1)
            dve.wait_ge(s_pwt, 1)
            ch.link(v.tensor_copy(comb1[:, :], bank[:, 1, 0:2 * P]))
            phase_end(dve, 4)
            with dve.Fori(0, B) as b:
                ch.enter(b, NE + 1)
                for x in range(NE):
                    dve.wait_ge(s_fo, NE * b + x + 1)
                    ye = bank[:, 6 + x % 2, :].rearrange("p (q d) -> p q d", q=TQ)
                    for q in range(TQ):
                        onto = acc[:, q, :] if x else h[:, ds(b * TQ + q, 1), :].rearrange("p a d -> p (a d)")
                        w = comb1[:, ds((q % 2) * P + x * NC + q // 2 + 2 * b, 1)]
                        last = v.scalar_tensor_tensor(acc[:, q, :], ye[:, q, :], w, onto, ALU.mult, ALU.add)
                    ch.link(last)
                    dve.nop().then_inc(s_foc, 1)
                ch.link(v.tensor_scalar(h[:, ds(b * TQ, TQ), :], acc[:, :, :], 1.0, None, ALU.mult))
            ch.leave(B)
            phase_end(dve, 5)

        @block.tensor
        def _(te):
            te.wait_ge(*consts_in)
            te.wait_ge(s_setup, 4)
            mm = te.matmul
            with te.Fori(0, B) as b:
                te.wait_ge(s_y, b + 1)
                for q in range(TQ):
                    last = te.transpose(bank[:, 0, q * P:(q + 1) * P], y[:, q, :], ident[:, :])
                last.then_inc(s_yt, 1)
                te.wait_ge(s_ytc, b + 1)
                mm(bank[:, 4, :], wq[:, :], yT[:, :], start=True, stop=True).then_inc(s_qkv, 1)
                mm(bank[:, 5, :], wk[:, :], yT[:, :], start=True, stop=True).then_inc(s_qkv, 1)
                for q in range(TQ):
                    last = mm(bank[:, 6 + q // 2, (q % 2) * 256:(q % 2) * 256 + 256], yT[:, q * P:(q + 1) * P],
                              wv[:, :], start=True, stop=True)
                last.then_inc(s_qkv, 1)
                for n in range(8):
                    p, to_k = n // 2, n % 2
                    te.wait_ge(s_split, 2 * b + 1 + to_k)
                    if n >= 2:
                        te.wait_ge(s_repc, 8 * b + n - 1)
                    for lo in range(2):
                        last = mm(bank[:, n % 2, :], spread[:, 2 * to_k + lo, p * P:(p + 1) * P],
                                  part[:, 2 * to_k + lo, :], start=(lo == 0), stop=(lo == 1))
                    last.then_inc(s_rep, 1)

                def scores1(g, n):
                    m = g * GH * TQ + n
                    h4, qt = n // TQ, n % TQ
                    if m >= 2:
                        te.wait_ge(s_max, NU1 * b + m - 1)
                    p, r = 2 * g + h4 // 2, 64 * (h4 % 2)
                    mm(bank[:, 2 + m % 2, :], q_rows[r:r + 64, p, qt * P:(qt + 1) * P],
                       k_rows[r:r + 64, p, :], start=True, stop=True).then_inc(s_s1, 1)

                def max_rows(g):
                    te.wait_ge(s_m, 2 * b + g + 1)
                    for pp in range(2):
                        if pp:
                            te.wait_ge(s_qm, 4 * b + 2 * g + 1)
                        for q in range(TQ):
                            last = mm(bank[:, 0, q * P:(q + 1) * P], max_cols[:, 2 * g + pp, q, :],
                                      ident_r[:, :], start=True, stop=True)
                        last.then_inc(s_mrow, 1)

                def scores2(u):
                    g, kt, pp = u // 8, (u % 8) // 2, u % 2
                    p = 2 * g + pp
                    te.wait_ge(s_qm, 4 * b + p + 1)
                    if u >= 2:
                        te.wait_ge(s_exp, NU2 * b + u - 1)
                    for hh in range(2):
                        r = 64 * hh
                        last = mm(bank[:, 4 + 2 * (u % 2) + hh, :], k_rows[r:r + 64, p, kt * P:(kt + 1) * P],
                                  qm_rows[r:r + 64, p, :], start=True, stop=True)
                    last.then_inc(s_s2, 1)

                def contexts(a):
                    g, kt = a // 4, a % 4
                    te.wait_ge(s_exp, NU2 * b + 2 * a + 2)
                    te.wait_ge(s_v, b + 1)
                    if kt == 0 and g:
                        te.wait_ge(s_ctx, 2 * b + g)
                    for h4 in range(GH):
                        last = mm(bank[32 * h4:32 * h4 + 32, 1, :],
                                  v_tok[:, kt, g * P + 32 * h4:g * P + 32 * h4 + 32],
                                  probs[:, (2 * a) % 4 + h4 // 2, h4 % 2, :],
                                  start=(kt == 0), stop=(kt == TQ - 1), tile_position=(0, 32 * h4))
                    last.then_inc(s_av, 1)

                def sums(g):
                    te.wait_ge(s_ctx, 2 * b + g + 1)
                    for q in range(TQ):
                        last = mm(bank[:, 0, g * TQ * GH + q * GH:g * TQ * GH + (q + 1) * GH],
                                  ctx_raw[:, g, q * P:(q + 1) * P], pick_sum[:, :], start=True, stop=True)
                    last.then_inc(s_sum, 1)
                    te.wait_ge(s_rec, 2 * b + g + 1)
                    if g:
                        te.wait_ge(s_cn, 2 * b + g)
                    for q in range(TQ):
                        last = mm(bank[:, 2, q * P:(q + 1) * P], recip_cols[:, q, :], ident[:, :],
                                  start=True, stop=True)
                    last.then_inc(s_bc, 1)

                for n in range(GH * TQ):
                    if n == 0:
                        te.wait_ge(s_repc, 8 * b + 8)
                    scores1(0, n)
                for n in range(EARLY):
                    scores1(1, n)
                max_rows(0)
                n = EARLY
                for u in range(8):
                    scores2(u)
                    while n < GH * TQ and n - EARLY < (u + 1) * 2:
                        scores1(1, n)
                        n += 1
                    if u % 2 == 1:
                        contexts(u // 2)
                max_rows(1)
                for u in range(8, 16):
                    scores2(u)
                    if u % 2 == 1:
                        contexts(u // 2)
                sums(0)
                sums(1)
                te.wait_ge(s_cn, 2 * b + 2)
                for q in range(TQ):
                    o = bank[:, 0, q * P:(q + 1) * P]
                    for g in range(NG):
                        mm(o, ctx_n[:, g, q * P:(q + 1) * P], wo[:, g, :], start=(g == 0), stop=False)
                    last = mm(o, ones_row[:, 0:P], bo_row[:, :], start=False, stop=True)
                last.then_inc(s_o, 1)
            phase_end(te, 0)
            if upto < 1:
                return

            te.wait_ge(s_weights0, 16 * len(WEIGHTS0))
            NX = 3 * NE + SHT
            with te.Fori(0, B) as b:
                te.wait_ge(s_by, b + 1)
                for q in range(TQ):
                    last = te.transpose(bank[:, 0, q * P:(q + 1) * P], y[:, q, :], ident[:, :])
                last.then_inc(s_byt, 1)
                te.wait_ge(s_bytc, b + 1)
                for q in range(TQ):
                    last = mm(bank[:, 1, q * NE:(q + 1) * NE], yT[:, q * P:(q + 1) * P], gate_w[:, :],
                              start=True, stop=True)
                last.then_inc(s_logit, 1)

                def down(x):
                    K = HT if x < NE else SHT
                    te.wait_ge(s_actv, NX * b + HT * x + K)
                    if x >= 2:
                        te.wait_ge(s_yec, (NE + 1) * b + x - 1)
                    for q in range(TQ):
                        for k in range(K):
                            w = w2[:, x, k, :] if x < NE else sw2[:, k, :]
                            last = mm(bank[:, 6 + x % 2, q * P:(q + 1) * P], act[:, x % 2, k, q * P:(q + 1) * P],
                                      w, start=(k == 0), stop=(k == K - 1))
                    last.then_inc(s_ye, 1)

                n = 0
                for x in range(NE + 1):
                    for k in range(HT if x < NE else SHT):
                        c = slice(k * P, (k + 1) * P)
                        if n >= 2:
                            te.wait_ge(s_actv, NX * b + n - 1)
                        s = 2 + 2 * (n % 2)
                        mm(bank[:, s, :], w1[:, x, c] if x < NE else sw1[:, c], yT[:, :], start=True, stop=True)
                        mm(bank[:, s + 1, :], w3[:, x, c] if x < NE else sw3[:, c], yT[:, :],
                           start=True, stop=True).then_inc(s_gu, 1)
                        n += 1
                    down(x)
            phase_end(te, 1)
            if upto < 2:
                return

            te.wait_ge(s_weights1, 16 * len(WEIGHTS1))
            te.wait_ge(s_setup, 9)
            with te.Fori(0, B) as b:
                te.wait_ge(s_cy, b + 1)
                for q in range(TQ):
                    last = te.transpose(bank[:, 0, q * P:(q + 1) * P], y[:, q, :], ident[:, :])
                last.then_inc(s_cyt, 1)
                for n, (m, bk) in enumerate(((3, 4), (1, 2), (2, 3), (0, 1))):
                    te.wait_ge(s_mix, 4 * b + n + 1)
                    mm(bank[:, bk, :], mix_w[:, m, :], mixed[:, m, :], start=True, stop=True).then_inc(s_proj, 1)
                mm(bank[:, 5, :], mix_w[:, 4, :], yT[:, :], start=True, stop=True).then_inc(s_proj, 1)
                te.wait_ge(s_kv_split, 3 * b + 3)
                mm(bank[:, 6, :], head_ones_r[:, :], part1[:, 2, :], start=True, stop=False)
                mm(bank[:, 6, :], head_ones_r[:, :], part1[:, 3, :], start=False, stop=True).then_inc(s_vsum, 1)

                def broadcasts(e):
                    if e >= 2:
                        te.wait_ge(s_vbc, DK * b + e - 1)
                    elif e == 0:
                        te.wait_ge(s_sig, 2 * b + 1)
                    for lo in range(2):
                        last = mm(bank[:, 1 + e % 2, :], pick[:, e, :], part1[:, 2 + lo, :],
                                  start=(lo == 0), stop=(lo == 1))
                    last.then_inc(s_vb, 1)
                    if e >= 2:
                        te.wait_ge(s_term, DK * b + e - 1)
                    elif e == 1:
                        te.wait_ge(s_w, 3 * b + 1)
                    for lo in range(2):
                        last = mm(bank[:, 3 + e % 2, :], pick[:, e, :], part1[:, lo, :],
                                  start=(lo == 0), stop=(lo == 1))
                    last.then_inc(s_kb, 1)

                def add_term(e):
                    te.wait_ge(s_term, DK * b + e + 1)
                    mm(bank[:, 7, :], ident[:, :], term[:, e % 2, :], start=(e == 0),
                       stop=(e == DK - 1)).then_inc(s_acc, 1)

                for e in range(DK):
                    broadcasts(e)
                    if e >= 2:
                        add_term(e - 2)
                add_term(DK - 2)
                add_term(DK - 1)
                te.wait_ge(s_gm, 2 * b + 1)
                te.wait_ge(s_sig, 2 * b + 2)
                mm(bank[:, 5, 0:1], head_ones[:, :], gn_mv[:, 0:1], start=True, stop=True).then_inc(s_gmr, 1)
                te.wait_ge(s_gm, 2 * b + 2)
                mm(bank[:, 5, 2:3], head_ones[:, :], gn_dev[:, :], start=True, stop=True).then_inc(s_gmr, 1)
                te.wait_ge(s_on, b + 1)
                for q in range(TQ):
                    last = mm(bank[:, 0, q * P:(q + 1) * P], wkv[:, q * P:(q + 1) * P], wout[:, :],
                              start=True, stop=True)
                last.then_inc(s_co, 1)
            phase_end(te, 2)
            if upto < 3:
                return

            te.wait_ge(s_weights2, 16 * len(WEIGHTS2))
            with te.Fori(0, B) as b:
                te.wait_ge(s_dy, b + 1)
                for q in range(TQ):
                    last = te.transpose(bank[:, 0, q * P:(q + 1) * P], y[:, q, :], ident[:, :])
                last.then_inc(s_dyt, 1)
                te.wait_ge(s_dytc, b + 1)
                mm(bank[0:NE, 1, :], router[:, :], yT[:, :], start=True, stop=True).then_inc(s_dl, 1)
                te.wait_ge(s_dlc, b + 1)
                te.wait_ge(s_dcopy, b + 1)
                te.nop()
            phase_end(te, 3)
            with te.Fori(0, 30) as i:
                te.wait_ge(s_cnt, i + 1)
                mm(bank[:, 0, 0:1], same_e[:, :], count[:, :], start=True, stop=True).then_inc(s_tot, 1)
            te.wait_ge(s_cnt, 31)
            mm(bank[:, 0, 1:2], same_e[:, :], count[:, :], start=True, stop=True).then_inc(s_tot, 1)
            te.wait_ge(s_cnt, 32)
            mm(bank[:, 0, 2:3], before[:, :], count[:, :], start=True, stop=True).then_inc(s_tot, 1)
            te.wait_ge(s_pw, 1)
            for n in range(2):
                last = te.transpose(bank[:, 1, n * P:(n + 1) * P], chosen[:, n * P:(n + 1) * P], ident[:, :])
            last.then_inc(s_pwt, 1)
            phase_end(te, 4)
            with te.Fori(0, B) as b:
                for x in range(NE):
                    for k in range(FT):
                        n = x * FT + k
                        if n >= 4:
                            te.wait_ge(s_gelu, NE * FT * b + n - 3)
                        elif n == 0:
                            te.wait_ge(s_phase[4], 4)
                        mm(bank[:, 2 + n % 4, :], f1[:, x, k * P:(k + 1) * P], yT_all[:, ds(b * T, T)],
                           start=True, stop=True).then_inc(s_up, 1)
                    te.wait_ge(s_gelu, NE * FT * b + (x + 1) * FT)
                    te.wait_ge(s_foc, NE * b + x + 1)
                    for q in range(TQ):
                        o = bank[:, 6 + x % 2, q * P:(q + 1) * P]
                        for k in range(FT):
                            mm(o, act[:, x % 2, k, q * P:(q + 1) * P], f2[:, x, k, :], start=(k == 0), stop=False)
                        last = mm(o, ones_row[:, 0:P], fb2_row[:, x * D:(x + 1) * D], start=False, stop=True)
                    last.then_inc(s_fo, 1)
            phase_end(te, 5)


def host_layout(x):
    import numpy as np

    f = np.float32
    c = np.ascontiguousarray
    D, NH, DK, T = 128, 8, 16, 512

    def pad_heads(w):
        o = np.zeros((w.shape[0], 2, 4, 32), f)
        o[..., :DK] = w.reshape(w.shape[0], 2, 4, DK)
        return o.reshape(w.shape[0], 256)

    pos = np.arange(T, dtype=f)[:, None]
    div = np.exp(np.arange(0, DK, 2, dtype=f) * f(-(np.log(10000.0) / DK)))
    ang = pos * div[None, :]
    pe = np.stack([np.sin(ang), np.cos(ang)], axis=-1).reshape(T, DK).astype(f)
    spread = np.zeros((128, 4, 4, 2, 64), f)
    for p in range(4):
        for hh in range(2):
            for d in range(DK):
                src = (2 * p + hh) * DK + d
                spread[src, 0, p, hh, [d, 2 * DK + d]] = 1
                spread[src, 1, p, hh, DK + d] = 1
                spread[src, 2, p, hh, [d, DK + d]] = 1
                spread[src, 3, p, hh, 2 * DK + d] = 1
    ones_rows = np.zeros((2, 64), f)
    ones_rows[:, 3 * DK:3 * DK + 2] = 1
    pick = np.zeros((128, 4), f)
    for j in range(4):
        pick[32 * j + DK, j] = 1
    bv = pad_heads(x["L0_attn_bv"].reshape(1, D))
    bv.reshape(8, 32)[:, DK] = 1
    zero = np.zeros(D, f)
    vec = c(np.stack([x["L0_attn_ln_g"], x["L0_attn_ln_b"], x["L0_attn_bq"], x["L0_attn_bk"],
                      ones_rows.reshape(-1), zero, zero, zero], axis=1))
    head = np.arange(128) // DK
    head_ones = (head[:, None] == head[None, :]).astype(f)
    pick_e = np.zeros((128, DK, 128), f)
    for e in range(DK):
        pick_e[:, e, :] = head_ones * (np.arange(128) % DK == e)[:, None]
    tri = np.tril(np.ones((8, 8), f), -1).reshape(1, 64)
    return {
        "x": c(x["x"].reshape(32, 128).T),
        "emb": c(x["L0_tok_W"].T),
        "tok_b": x["L0_tok_b"],
        "vec": vec,
        "ident": np.eye(128, dtype=f),
        "wq": c(x["L0_attn_wq"].T), "wk": c(x["L0_attn_wk"].T),
        "wv": pad_heads(c(x["L0_attn_wv"].T)),
        "wo": c(pad_heads(x["L0_attn_wo"]).T.reshape(2, 128, 128)),
        "bo": x["L0_attn_bo"].reshape(1, D), "bv": bv.reshape(256),
        "pe": c(np.tile(pe.T, (NH, 1))),
        "spread": spread.reshape(128, 4, 512),
        "pick_sum": pick,
        "gate_w": c(x["L0_ffn_gate_w"].T),
        "w1": c(x["L0_ffn_w1"].transpose(0, 2, 1)), "w3": c(x["L0_ffn_w3"].transpose(0, 2, 1)),
        "w2": c(x["L0_ffn_w2"].transpose(0, 2, 1)),
        "sw1": c(x["L0_ffn_sw1"].T), "sw3": c(x["L0_ffn_sw3"].T), "sw2": c(x["L0_ffn_sw2"].T),
        "tri": tri.reshape(64),
        "mix_w": c(np.stack([x["L1_attn_" + n].T for n in ("Wr", "Wk", "Wv", "Ww", "Wg")])),
        "wout": c(x["L1_attn_Wout"].T),
        "vec1": c(np.stack([x["L1_attn_" + n].reshape(-1) for n in
                            ("mu_r", "mu_k", "mu_v", "mu_w", "decay_A", "decay_B", "decay_base", "u",
                             "gn_w", "gn_b")], axis=1)),
        "pick": pick_e.reshape(128, 2048),
        "head_ones": head_ones,
        "router": x["L1_ffn_Wr"], "f1": x["L1_ffn_W1"], "f2": x["L1_ffn_W2"],
        "fb1": c(x["L1_ffn_b1"].reshape(32, 128).T), "fb2": x["L1_ffn_b2"].reshape(1, 1024),
        "bits": np.tile((1 << np.arange(29, -1, -1)).astype(np.int32), (128, 1)),
        "before": c(head_ones * np.triu(np.ones((128, 128), f), 1)),
    }


def kernel(**inputs):
    import numpy as _np
    import concourse.bacc as _bacc
    from concourse import mybir as _mybir
    from concourse.bass_utils import run_bass_kernel_spmd as _run

    nc = _bacc.Bacc("TRN2", target_bir_lowering=False, num_devices=1)
    laid = host_layout({k: _np.asarray(v) for k, v in inputs.items()})
    arrays = {f"in_{k}": v for k, v in laid.items()}
    aps = {k: nc.dram_tensor(f"in_{k}", v.shape, _mybir.dt.from_np(v.dtype), kind="ExternalInput").ap()
           for k, v in laid.items()}
    out = nc.dram_tensor("out", (8, 512, 128), _mybir.dt.float32, kind="ExternalOutput").ap()
    lm_tower(nc, aps, out)
    r = _run(nc, [arrays], core_ids=[0])
    return r.results[0]["out"]
```

```python
import concourse.bass as bass
from concourse import mybir
from contextlib import ExitStack


class Chain:

    def __init__(self, eng, sem):
        self.eng, self.sem, self.base, self.n = eng, sem, 0, 0

    def step(self, ins):
        ins.then_inc(self.sem, 1)
        self.n += 1

    def wait(self, apart=None):
        self.eng.wait_ge(self.sem, self.base + self.n)
        if apart is not None:
            self.eng.nop().then_inc(apart, 1)

    def link(self, ins, apart=None):
        self.step(ins)
        self.wait(apart)

    def enter(self, i, per):
        self.start, self.per = self.base + self.n, per
        self.base, self.n = self.start + i * per, 0

    def leave(self, turns):
        assert self.n == self.per, f"{self.n} steps a turn, not {self.per}"
        self.base, self.n = self.start + turns * self.per, 0


def wait(eng, sem, value):
    if not (isinstance(value, int) and value <= 0):
        eng.wait_ge(sem, value)


def turns(eng, n, body, last=False):
    body(0)
    with eng.Fori(1, n - last) as i:
        body(i)
    if last:
        body(n - 1)


def lm_tower(nc, t, out, upto=3):
    fp32, f32r, i32 = mybir.dt.float32, mybir.dt.float32r, mybir.dt.int32
    ALU, ACT, AX = mybir.AluOpType, mybir.ActivationFunctionType, mybir.AxisListType.X
    ds = bass.ds

    P = 128
    B, T, D = 8, 512, 128
    NT = B * T // P
    TQ = T // P
    NH, DK = 8, 16
    VOCAB = t["emb"].shape[0]
    EPS = 1e-5
    NE, HID, TOPK = 8, 384, 2
    HT = HID // P
    FT = t["f1"].shape[2] // P
    CAP = 1024
    SH = CAP // P
    NB = NE * CAP // T
    bf16 = mybir.dt.bfloat16
    SHT = t["sw1"].shape[1] // P
    XT = (TOPK * B * T // P + NE) // (2 * TQ) * (2 * TQ)
    assert XT >= TOPK * B * T // P + NE - 1
    XG = XT // TQ
    SCALE = DK ** -0.5
    GH = 4
    NG = NH // GH

    ctx = ExitStack()
    with ctx:
        space = ctx

        def sb(name, shape, dt=fp32):
            return space.enter_context(nc.sbuf_tensor(name, shape, dt))

        def sem(name):
            return ctx.enter_context(nc.semaphore(name))

        y_rows = nc.dram_tensor("y_rows", (B * T, D), fp32, kind="Internal").ap()
        x_slots = nc.dram_tensor("x_slots", (XT * P, D), fp32, kind="Internal").ap()
        e_slots = nc.dram_tensor("e_slots", (XT * P, D), fp32, kind="Internal").ap()
        out_flat = out.rearrange("b t d -> (b t) d")
        bank = ctx.enter_context(nc.psum_tensor("bank", [P, 8, 512], fp32))

        h = sb("h", [P, NT, D])
        ident = sb("ident", [P, P])
        ident_r = sb("ident_r", [P, P], f32r)
        ones_row = sb("ones_row", [1, 512])
        half_neg = sb("half_neg", [P, NT])
        token_id = sb("token_id", [P, NT], i32)
        tok_b = sb("tok_b", [P, D])
        stats = sb("stats", [P, NT, 6])
        mv = sb("mv", [P, NT, 2])
        var_eps = sb("var_eps", [P, NT])
        rstd = sb("rstd", [P, NT])
        rstd2 = sb("rstd2", [P, NT])
        y = sb("y", [P, TQ, D])
        yT = sb("yT", [P, T])

        gate_w = sb("gate_w", [P, NE])
        w1, w3 = sb("w1", [P, NE, HID]), sb("w3", [P, NE, HID])
        w2 = sb("w2", [P, NE, HT, D])
        sw1, sw3, sw2 = sb("sw1", [P, SHT * P]), sb("sw3", [P, SHT * P]), sb("sw2", [P, SHT, D])
        tri = sb("tri", [P, NE, NE])
        gated = sb("gated", [P, 2, T])
        act = sb("act", [P, SHT + 2, T])

        lent = ExitStack()
        space = lent
        vec = sb("vec", [P, 8])
        wq, wk, wv = sb("wq", [P, D]), sb("wk", [P, D]), sb("wv", [P, D])
        wo = sb("wo", [P, NG, D])
        bo_row = sb("bo_row", [1, D])
        bv = sb("bv", [P, D])
        pe = sb("pe", [P, T])
        spread_f = sb("spread_f", [P, 4, 4 * P])
        spread = sb("spread", [P, 4, 4 * P], f32r)
        pick_sum = sb("pick_sum", [P, GH])
        part = sb("part", [P, 4, T], f32r)
        k_full = sb("k_full", [P, T])
        q_rows = sb("q_rows", [P, 4, T], f32r)
        qm_rows = sb("qm_rows", [P, 2, 4, T], f32r)
        k_rows = sb("k_rows", [P, 2, 4, T], f32r)
        v_tok = sb("v_tok", [P, 2, TQ, NH * 32])
        neg_max = sb("neg_max", [P, NG, TQ, GH])
        max_cols = sb("max_cols", [P, 4, TQ, P], f32r)
        probs = sb("probs", [P, 4, 2, T])
        ctx_raw = sb("ctx_raw", [P, NG, T])
        ctx_n = sb("ctx_n", [P, NG, T])
        recip = sb("recip", [P, NG * TQ * GH])
        recip_cols = sb("recip_cols", [P, NG, TQ, P])

        lent.close()
        space = ctx

        mix_w = sb("mix_w", [P, 5, D])
        wout = sb("wout", [P, D])
        vec1 = sb("vec1", [P, 10])
        keep_mu = sb("keep_mu", [P, 4])
        pick = sb("pick", [P, DK, P], f32r)
        pick_f = act[:, 0:4, :].rearrange("p k n -> p (k n)")
        head_ones = sb("head_ones", [P, P])
        head_ones_r = sb("head_ones_r", [P, P], f32r)

        lent = ExitStack()
        space = lent
        y_all, yT_all = sb("y_all", [P, NT, D]), sb("yT_all", [P, B * T])
        logit, score = sb("logit", [P, NT, NE]), sb("score", [P, NT, NE])
        top = sb("top", [P, NT])
        better, tied = sb("better", [P, NT, NE, NE]), sb("tied", [P, NT, NE, NE])
        rank_e = sb("rank_e", [P, NT, NE])
        sel = sb("sel", [P, TOPK, NT, NE])
        chosen_e = sb("chosen_e", [P, NE, NT])
        strict, all_ones = sb("strict", [P, P]), sb("all_ones", [P, P])
        goes_on = sb("goes_on", [P, NE, NT])
        total, upto_tile = sb("total", [P, NE, NT]), sb("upto_tile", [P, NE, NT])
        place_e = sb("place_e", [P, NE, NT])
        taken = sb("taken", [P, NE])
        taken_i = sb("taken_i", [P, NE], i32)
        tiles_of, tile_end, row_base = sb("tiles_of", [P, NE]), sb("tile_end", [P, NE]), sb("row_base", [P, NE])
        picked_e = sb("picked_e", [P, TOPK, NT, NE])
        row_f, row_id = sb("row_f", [P, TOPK, NT]), sb("row_id", [P, TOPK, NT], i32)
        weight = sb("weight", [P, TOPK, NT])
        tile_up = sb("tile_up", [1, XT])
        past = sb("past", [1, XT, NE])
        owner_f, owner = sb("owner_f", [1, XT]), sb("owner", [1, XT], i32)
        x_rows = sb("x_rows", [P, 2, TQ, D])
        turned = sb("turned", [P, 4, HT + 1, P])
        e_rows = sb("e_rows", [P, 2, TQ, D])
        back = sb("back", [P, 2, TQ, TOPK, D])
        lent.close()
        space = ctx

        router = sb("router", [P, NE])
        f1 = sb("f1", [P, 2, FT * P])
        f2 = sb("f2", [P, 2, FT, D])
        fb1 = sb("fb1", [P, NE * FT])
        fb2_row = sb("fb2_row", [1, NE * D])
        bits = sb("bits", [P, 30], i32)
        same_e, before = sb("same_e", [P, P]), sb("before", [P, P])

        lent = ExitStack()
        space = lent
        x_star = sb("x_star", [P, T])
        mixed = sb("mixed", [P, 4, T])
        k1 = sb("k1", [P, 2, T])
        part1 = sb("part1", [P, 2, 4, T], f32r)
        decay = sb("decay", [P, 2, T])
        sig_r, sig_g = sb("sig_r", [P, 2, T]), sb("sig_g", [P, 2, T])
        bonus = sb("bonus", [P, 2, T])
        v_all = sb("v_all", [P, 2, T])
        kv = sb("kv", [P, 2, T])
        fwd, bwd = sb("fwd", [P, 2, T + 1]), sb("bwd", [P, 2, T + 1])
        both = sb("both", [P, 2, T])
        term = sb("term", [P, 2, T])
        wkv = sb("wkv", [P, T])
        gn_stat, gn_mv = sb("gn_stat", [P, 6]), sb("gn_mv", [P, 2])
        gn_mean, gn_dev, gn_var = sb("gn_mean", [P, 1]), sb("gn_dev", [P, 1]), sb("gn_var", [P, 1])
        gn_rstd, gn_gain, gn_off = sb("gn_rstd", [P, 1]), sb("gn_gain", [P, 1]), sb("gn_off", [P, 1])

        lent.close()
        space = ctx

        lg = sb("lg", [NE, B * T])
        NC = P // NE
        CW = B * T // NC
        prob = sb("prob", [P, CW])
        part_top, part_sum, rsum = sb("part_top", [P, 1]), sb("part_sum", [P, 1]), sb("rsum", [P, 1])
        expert_top, top_row, neg_top = sb("expert_top", [1, NE]), sb("top_row", [1, NE, NC]), sb("neg_top", [P, 1])
        thr, cand, keep = sb("thr", [P, 1], i32), sb("cand", [P, 1], i32), sb("keep", [P, 1], i32)
        hit, rank, ones_cw = sb("hit", [P, CW]), sb("rank", [P, CW]), sb("ones_cw", [P, CW])
        count, need = sb("count", [P, 1]), sb("need", [P, 1])
        chosen = sb("chosen", [P, CW])
        comb1 = sb("comb1", [P, 2 * P])
        slot = sb("slot", [P, CW])
        slot_i, low_i = sb("slot_i", [P, 2 * P], i32), sb("low_i", [P, 2 * P], i32)
        slot_lo, slot_hi = sb("slot_lo", [P, 2 * P]), sb("slot_hi", [P, 2 * P])
        tile_no = sb("tile_no", [P, 2 * P])
        count_up = sb("count_up", [P, P])
        row_no = sb("row_no", [P, 1])
        w_a, w_b, w_c = (sb("w_a", [P, 2 * P], bf16), sb("w_b", [P, 2 * P], bf16), sb("w_c", [P, 2 * P], bf16))
        w_rest = sb("w_rest", [P, 2 * P])
        in_hi = sb("in_hi", [P, 2 * P, SH])
        entry = sb("entry", [P, 2 * P, 5, SH], bf16)
        onehot = sb("onehot", [P, 2, 2 * NE, P], bf16)
        zeros = sb("zeros", [P, NE * 5 * SH], bf16)
        list_raw = sb("list_raw", [P, NE, 5, SH])
        list_f = sb("list_f", [P, NE, SH])
        list_id = sb("list_id", [P, NE * SH], i32)
        list_w = sb("list_w", [P, NE, SH])
        now_id = sb("now_id", [P, 4, TQ], i32)
        picked = sb("picked", [P, 2, TQ, D])
        pickedT = sb("pickedT", [P, 2, T])
        out_rows = sb("out_rows", [P, 2, TQ, D])

        s_const = sem("s_const")
        s_weights0 = sem("s_weights0")
        s_setup = sem("s_setup")
        s_emb = [sem(f"s_emb{b}") for b in range(B)]
        s_apart, s_apart_act, s_apart_pool = sem("s_apart"), sem("s_apart_act"), sem("s_apart_pool")
        s_apart_te = sem("s_apart_te")
        s_dve, s_act, s_pool = sem("s_dve"), sem("s_act"), sem("s_pool")
        s_out = sem("s_out")
        s_phase = [sem(f"s_phase{n}") for n in range(6)]

        s_var, s_rstd, s_var2, s_rstd2 = sem("s_var"), sem("s_rstd"), sem("s_var2"), sem("s_rstd2")
        s_y, s_yt, s_ytc = sem("s_y"), sem("s_yt"), sem("s_ytc")
        s_qkv, s_split, s_v = sem("s_qkv"), sem("s_split"), sem("s_v")
        s_rep, s_repc = sem("s_rep"), sem("s_repc")
        s_s1, s_max, s_m = sem("s_s1"), sem("s_max"), sem("s_m")
        s_mrow, s_qm = sem("s_mrow"), sem("s_qm")
        s_s2, s_exp, s_av = sem("s_s2"), sem("s_exp"), sem("s_av")
        s_ctx, s_sum, s_rec, s_bc, s_cn = sem("s_ctx"), sem("s_sum"), sem("s_rec"), sem("s_bc"), sem("s_cn")
        s_o = sem("s_o")

        s_bvar, s_brstd = sem("s_bvar"), sem("s_brstd")
        s_by, s_byt, s_bytc = sem("s_by"), sem("s_byt"), sem("s_bytc")
        s_logit, s_logc, s_escore = sem("s_logit"), sem("s_logc"), sem("s_escore")
        s_zeroed, s_cleared, s_routing = sem("s_zeroed"), sem("s_cleared"), sem("s_routing")
        s_before, s_total, s_rows, s_owner = sem("s_before"), sem("s_total"), sem("s_rows"), sem("s_owner")
        s_dispatch = sem("s_dispatch")
        s_gu, s_silu, s_actv, s_ye, s_yec = sem("s_gu"), sem("s_silu"), sem("s_actv"), sem("s_ye"), sem("s_yec")
        s_xload = [sem("s_xload0"), sem("s_xload1")]
        s_estore = [sem("s_estore0"), sem("s_estore1")]
        s_eup, s_esilu, s_eact, s_tr, s_trc = sem("s_eup"), sem("s_esilu"), sem("s_eact"), sem("s_tr"), sem("s_trc")
        s_edown, s_erows = sem("s_edown"), sem("s_erows")
        s_back = [sem("s_back0"), sem("s_back1")]
        s_added = sem("s_added")

        s_cvar, s_crstd = sem("s_cvar"), sem("s_crstd")
        s_cy, s_cyt, s_cytc, s_star = sem("s_cy"), sem("s_cyt"), sem("s_cytc"), sem("s_star")
        s_mix, s_proj, s_hi, s_lo = sem("s_mix"), sem("s_proj"), sem("s_hi"), sem("s_lo")
        s_mu, s_w, s_sig, s_vsum = sem("s_mu"), sem("s_w"), sem("s_sig"), sem("s_vsum")
        s_vb, s_vbc, s_kv, s_kb = sem("s_vb"), sem("s_vbc"), sem("s_kv"), sem("s_kb")
        s_scan, s_both, s_term, s_acc = sem("s_scan"), sem("s_both"), sem("s_term"), sem("s_acc")
        s_gm, s_gmr, s_gvar, s_grstd, s_on, s_co = (sem("s_gm"), sem("s_gmr"), sem("s_gvar"), sem("s_grstd"),
                                                    sem("s_on"), sem("s_co"))
        s_wkv = sem("s_wkv")
        s_weights1, s_weights2 = sem("s_weights1"), sem("s_weights2")

        s_dvar, s_drstd = sem("s_dvar"), sem("s_drstd")
        s_dy, s_dyt, s_dytc = sem("s_dy"), sem("s_dyt"), sem("s_dytc")
        s_dl, s_dlc = sem("s_dl"), sem("s_dlc")
        s_spread, s_ptop, s_ptopt, s_etop, s_ebias, s_top = (sem("s_spread"), sem("s_ptop"), sem("s_ptopt"), sem("s_etop"),
                                                             sem("s_ebias"), sem("s_top"))
        s_pexp, s_psum = sem("s_pexp"), sem("s_psum")
        s_cnt, s_tot = sem("s_cnt"), sem("s_tot")
        s_up, s_gelu, s_fo = sem("s_up"), sem("s_gelu"), sem("s_fo")
        s_ystore = [sem("s_ystore0"), sem("s_ystore1")]
        s_slots, s_slotst, s_zero = sem("s_slots"), sem("s_slotst"), sem("s_zero")
        s_entry, s_hot, s_hotc, s_lists = sem("s_entry"), sem("s_hot"), sem("s_hotc"), sem("s_lists")
        s_load = [sem("s_load0"), sem("s_load1")]
        s_gather = [sem("s_gather0"), sem("s_gather1")]
        s_scatter = [sem("s_scatter0"), sem("s_scatter1")]
        s_xt, s_xtc, s_wy, s_now = sem("s_xt"), sem("s_xtc"), sem("s_wy"), sem("s_now")

        WEIGHTS1 = [(pick_f, t["pick"]), (mix_w[:, :, :], t["mix_w"].rearrange("m c d -> c m d")), (wout[:, :], t["wout"]),
                    (vec1[:, :], t["vec1"]), (head_ones[:, :], t["head_ones"])]
        WEIGHTS2 = [(router[:, :], t["router"]),
                    (fb1[:, :], t["fb1"]), (fb2_row[:, :], t["fb2"]), (bits[:, :], t["bits"]),
                    (same_e[:, :], t["head_ones"]), (before[:, :], t["before"]), (tile_no[:, :], t["tile_no"]),
                    (count_up[:, :], t["count_up"]), (row_no[:, :], t["row_no"])]
        CONSTS = [(vec[:, :], t["vec"]), (ident[:, :], t["ident"]), (wq[:, :], t["wq"]), (wk[:, :], t["wk"]),
                  (wv[:, :], t["wv"]), (wo[:, :, :], t["wo"].rearrange("g p n -> p g n")),
                  (bo_row[:, :], t["bo"]), (bv[:, :], t["bv"].partition_broadcast(P)),
                  (pe[:, :], t["pe"]), (spread_f[:, :, :], t["spread"]), (pick_sum[:, :], t["pick_sum"]),
                  (tok_b[:, :], t["tok_b"].partition_broadcast(P)), (token_id[:, :], t["x"])]
        WEIGHTS0 = [(gate_w[:, :], t["gate_w"]), (w1[:, :, :], t["w1"].rearrange("e d f -> d e f")),
                    (w3[:, :, :], t["w3"].rearrange("e d f -> d e f")),
                    (w2[:, :, :, :], t["w2"].rearrange("e (k p) d -> p e k d", p=P)),
                    (sw1[:, :], t["sw1"]), (sw3[:, :], t["sw3"]),
                    (sw2[:, :, :], t["sw2"].rearrange("(k p) d -> p k d", p=P)),
                    (tri[:, :, :], t["tri"].partition_broadcast(P))]
        ROUTING = [(strict[:, :], t["strict"]), (tile_up[:, :], t["tile_up"])]
        zero_rows = act[:, 0:3, :].rearrange("p k n -> p (k n)")[:, 0:XT * D // 8]
        consts_in = (s_const, 16 * len(CONSTS))

        def phase_end(eng, n):
            eng.nop().then_inc(s_phase[n], 1)
            eng.wait_ge(s_phase[n], 4)

        def maxima(p, hh):
            return 64 * hh + 3 * DK

        NQ = GH * TQ
        NU1, NU2 = NG * NQ, NG * TQ * 2

        block = ctx.enter_context(nc.Block())

        @block.sync
        def _(sp):
            for dst, src in CONSTS:
                sp.dma_start(dst, src).then_inc(s_const, 16)
            for b in range(B):
                sp.wait_ge(s_emb[b], 16 * TQ)
            for dst, src in WEIGHTS0:
                sp.dma_start(dst, src).then_inc(s_weights0, 16)
            sp.wait_ge(s_zeroed, 1)
            sp.dma_start(x_slots.rearrange("(p n r) d -> p n (r d)", p=P, n=8),
                         zero_rows[:, None, :].broadcast_to([P, 8, XT * D // 8])).then_inc(s_cleared, 16)
            sp.wait_ge(s_phase[0], 4)
            for dst, src in ROUTING:
                sp.dma_start(dst, src).then_inc(s_routing, 16)
            for dst, src in WEIGHTS1[1:]:
                sp.dma_start(dst, src).then_inc(s_weights1, 16)
            sp.wait_ge(s_dispatch, 16 * TOPK * NT)

            def load_rows(i, par):
                g = 2 * i + par
                wait(sp, s_tr, TQ * (g - 1))
                sp.dma_start(x_rows[:, par, :, :], x_in[:, ds(g * TQ, TQ), :]).then_inc(s_xload[par], 16)

            def store_rows(g, par):
                sp.wait_ge(s_erows, g + 1)
                sp.dma_start(e_out[:, ds(g * TQ, TQ), :], e_rows[:, par, :, :]).then_inc(s_estore[par], 16)

            x_in, e_out = (a.rearrange("(t p) d -> p t d", p=P) for a in (x_slots, e_slots))

            def tiles(i):
                for par in range(2):
                    load_rows(i, par)
                    if not isinstance(i, int) or i:
                        store_rows(2 * i + par - 2, par)

            turns(sp, XG // 2, tiles)
            for par in range(2):
                store_rows(XG - 2 + par, par)
            for par in range(2):
                sp.wait_ge(s_estore[par], 16 * (XG // 2 + par))
            sp.wait_ge(s_phase[1], 4)
            sp.dma_start(*WEIGHTS1[0]).then_inc(s_weights1, 16)
            if upto < 3:
                sp.wait_ge(s_phase[upto], 4)
                sp.dma_start(out.rearrange("b (j p) d -> p (b j) d", p=P), h[:, :, :]).then_inc(s_out, 16)
                sp.wait_ge(s_out, 16)
                return
            sp.wait_ge(s_phase[2], 4)
            for dst, src in WEIGHTS2:
                sp.dma_start(dst, src).then_inc(s_weights2, 16)
            sp.dma_start(out.rearrange("b (j p) d -> p (b j) d", p=P), h[:, :, :]).then_inc(s_out, 16)
            rows = y_rows.rearrange("(j p) d -> p j d", p=P)
            for b in range(B):
                sp.wait_ge(s_dy, b + 1)
                sp.dma_start(rows[:, b * TQ:(b + 1) * TQ, :], picked[:, b % 2, :, :]).then_inc(s_ystore[b % 2], 16)
            sp.wait_ge(s_dlc, B)
            sp.dma_start(prob[:, :], lg[:, :].rearrange("e (c n) -> e c n", c=NC)).then_inc(s_spread, 16)

            def load(i):
                for par in range(2):
                    wait(sp, s_fo, 4 * i + 2 * par - 2)
                    e = 2 * i + par
                    sp.dma_start(f1[:, par, :], t["f1"][ds(e, 1), :, :].rearrange("e d f -> d (e f)"))\
                      .then_inc(s_load[par], 16)
                    sp.dma_start(f2[:, par, :, :], t["f2"][ds(e, 1), :, :].rearrange("e (k p) d -> p (e k) d", p=P))\
                      .then_inc(s_load[par], 16)

            turns(sp, NE // 2, load)
            for half in range(2):
                sp.wait_ge(s_scatter[half], 16 * TQ * NB // 2)
            sp.wait_ge(s_out, 16)


        @block.gpsimd
        def _(pool):
            pool.memset(h[:, :, :], 0.0).then_inc(s_pool, 1)
            pool.memset(half_neg[:, :], -0.5).then_inc(s_pool, 1)
            pool.memset(zero_rows, 0.0).then_inc(s_zeroed, 1)
            pool.wait_ge(s_pool, 2)
            pool.wait_ge(*consts_in)

            def embed(b):
                for j in range(b * TQ, (b + 1) * TQ):
                    pool.indirect_dma_start(
                        out=h[:, j, :], out_offset=None, in_=t["emb"],
                        in_offset=bass.IndirectOffsetOnAxis(ap=token_id[:, j:j + 1], axis=0),
                        bounds_check=VOCAB - 1, oob_is_err=False).then_inc(s_emb[b], 16)

            def rsqrt(b, into, asked, done):
                c = slice(b * TQ, (b + 1) * TQ)
                pool.wait_ge(asked, b + 1)
                pool.tensor_tensor(into[:, c], var_eps[:, c], half_neg[:, c], ALU.pow).then_inc(done, 1)

            embed(0)
            embed(1)
            rsqrt(0, rstd, s_var, s_rstd)
            embed(2)
            rsqrt(0, rstd2, s_var2, s_rstd2)
            for b in range(3, B):
                embed(b)
            for b in range(1, B):
                rsqrt(b, rstd, s_var, s_rstd)
            for b in range(1, B):
                rsqrt(b, rstd2, s_var2, s_rstd2)
            phase_end(pool, 0)
            if upto < 1:
                return

            pool.memset(all_ones[:, :], 1.0).then_inc(s_setup, 1)
            pool.memset(goes_on[:, :, :], 1.0).then_inc(s_pool, 1)
            pool.wait_ge(s_pool, 3)
            pool.memset(goes_on[:, :, 0:1], 0.0).then_inc(s_setup, 1)
            for b in range(B):
                rsqrt(b, rstd, s_bvar, s_brstd)
            pool.wait_ge(s_rows, 1)
            pool.wait_ge(s_cleared, 16)
            for j in range(NT):
                for k in range(TOPK):
                    pool.indirect_dma_start(
                        out=x_slots, out_offset=bass.IndirectOffsetOnAxis(ap=row_id[:, k, j:j + 1], axis=0),
                        in_=y_all[:, j, :], in_offset=None, bounds_check=XT * P - 1).then_inc(s_dispatch, 16)
            for par in range(2):
                pool.wait_ge(s_estore[par], 16 * (XG // 2 + par))
            for b in range(B):
                if b >= 2:
                    pool.wait_ge(s_added, b - 1)
                for q in range(TQ):
                    for k in range(TOPK):
                        pool.indirect_dma_start(
                            out=back[:, b % 2, q, k, :], out_offset=None, in_=e_slots,
                            in_offset=bass.IndirectOffsetOnAxis(ap=row_id[:, k, b * TQ + q:b * TQ + q + 1], axis=0),
                            bounds_check=XT * P - 1, oob_is_err=False).then_inc(s_back[b % 2], 16)
            phase_end(pool, 1)
            if upto < 2:
                return


            def token_rstd(b):
                pool.wait_ge(s_cvar, b + 1)
                pool.tensor_tensor(rstd[:, 0:TQ], var_eps[:, 0:TQ], half_neg[:, 0:TQ], ALU.pow).then_inc(s_crstd, 1)

            def turn(b, bg, par):
                for e in range(DK):
                    if e == 1 and not (isinstance(b, int) and b == B - 1):
                        token_rstd(b + 1)
                    pool.wait_ge(s_vbc, DK * b + e + 1)
                    wait(pool, s_scan, DK * b + e - 1)
                    pool.tensor_tensor(kv[:, e % 2, :], k1[:, par, :], v_all[:, e % 2, :], ALU.mult).then_inc(s_kv, 1)
                    if e:
                        add_directions(b, e - 1)
                    elif bg is not None:
                        add_directions(bg, DK - 1)
                    if e == 7 and bg is not None:
                        group_rstd(bg)

            def add_directions(b, e):
                pool.wait_ge(s_scan, DK * b + e + 1)
                wait(pool, s_term, DK * b + e - 1)
                pool.tensor_tensor(both[:, e % 2, :], fwd[:, e % 2, 0:T], bwd[:, e % 2, 1:T + 1],
                                   ALU.add).then_inc(s_both, 1)

            def group_rstd(b):
                pool.wait_ge(s_gvar, b + 1)
                pool.tensor_tensor(gn_rstd[:, :], gn_var[:, :], half_neg[:, 0:1], ALU.pow).then_inc(s_grstd, 1)

            token_rstd(0)
            turn(0, None, 0)
            with pool.Fori(0, B // 2 - 1) as i:
                turn(2 * i + 1, 2 * i, 1)
                turn(2 * i + 2, 2 * i + 1, 0)
            turn(B - 1, B - 2, 1)
            add_directions(B - 1, DK - 1)
            group_rstd(B - 1)
            phase_end(pool, 2)
            if upto < 3:
                return

            for b in range(B):
                rsqrt(b, rstd, s_dvar, s_drstd)
            phase_end(pool, 3)
            phase_end(pool, 4)

            def gather(i, m):
                n = 4 * i + m
                pool.wait_ge(s_lists, 1)
                wait(pool, s_xt, n - 1)
                if not (isinstance(n, int) and n < 4):
                    pool.nop().then_inc(s_apart_pool, 1)
                    pool.wait_ge(s_scatter[m % 2], 16 * TQ * (2 * i + m // 2 - 1))
                pool.nop().then_inc(s_apart_pool, 1)
                pool.tensor_copy(now_id[:, m, :], list_id[:, ds(n * TQ, TQ)]).then_inc(s_now, 1)
                pool.wait_ge(s_now, n + 1)
                pool.nop().then_inc(s_apart_pool, 1)
                for q in range(TQ):
                    pool.indirect_dma_start(
                        out=picked[:, m % 2, q, :], out_offset=None, in_=y_rows,
                        in_offset=bass.IndirectOffsetOnAxis(ap=now_id[:, m, q:q + 1], axis=0),
                        bounds_check=B * T - 1, oob_is_err=False).then_inc(s_gather[m % 2], 16)

            def scatter(i, m):
                n = 4 * i + m
                if m % 2 == 0:
                    for half in range(2):
                        wait(pool, s_scatter[half], 16 * TQ * (2 * i + m // 2))
                        pool.nop().then_inc(s_apart_pool, 1)
                pool.wait_ge(s_wy, n + 1)
                pool.nop().then_inc(s_apart_pool, 1)
                for q in range(TQ):
                    pool.indirect_dma_start(
                        out=out_flat, out_offset=bass.IndirectOffsetOnAxis(ap=now_id[:, m % 4, q:q + 1], axis=0),
                        in_=out_rows[:, m % 2, q, :], in_offset=None, bounds_check=B * T - 1,
                        compute_op=ALU.add).then_inc(s_scatter[m % 2], 16)

            for par in range(2):
                pool.wait_ge(s_ystore[par], 16 * B // 2)
            pool.wait_ge(s_out, 16)

            def experts(i):
                for m in range(4):
                    gather(i, m)
                    if not (isinstance(i, int) and m < 2):
                        scatter(i, m - 2)

            turns(pool, NE // 2, experts)
            scatter(NE // 2, -2)
            scatter(NE // 2, -1)
            phase_end(pool, 5)

        @block.scalar
        def _(act_e):
            act_e.wait_ge(*consts_in)

            def turn(by, bx, par):
                for u in range(NU2):
                    if by is not None:
                        exponentials(by, u)
                        if u == 9:
                            contexts_out(by, 0)
                    if bx is not None:
                        if u == 0:
                            act_e.wait_ge(s_yt, bx + 1)
                            nc.scalar.activation(yT[:, :], bank[:, 0, :], ACT.Identity, bias=vec[:, 1:2],
                                                 scale=vec[:, 0:1]).then_inc(s_ytc, 1)
                        elif 2 <= u < 6:
                            rows_of_heads(bx, 1 - par, u - 2)
                if by is not None:
                    contexts_out(by, 1)

            def exponentials(b, u):
                a = u // 2
                act_e.wait_ge(s_s2, NU2 * b + u + 1)
                if a >= 2:
                    act_e.wait_ge(s_av, 8 * b + a - 1)
                s = 4 + 2 * (u % 2)
                nc.scalar.activation(probs[:, u % 4, :, :], bank[:, s:s + 2, :], ACT.Exp,
                                     scale=SCALE).then_inc(s_exp, 1)

            def contexts_out(b, g):
                act_e.wait_ge(s_av, 8 * b + 4 * g + 4)
                nc.scalar.activation(ctx_raw[:, g, :], bank[:, 1, :], ACT.Copy).then_inc(s_ctx, 1)

            def rows_of_heads(b, par, p):
                wait(act_e, s_qm, 4 * b)
                act_e.wait_ge(s_rep, 8 * b + 2 * p + 1)
                nc.scalar.activation(q_rows[:, p, :], bank[:, 2, :], ACT.Copy).then_inc(s_repc, 1)
                act_e.wait_ge(s_rep, 8 * b + 2 * p + 2)
                nc.scalar.activation(k_rows[:, par, p, :], bank[:, 3, :], ACT.Identity,
                                     bias=vec[:, 4:5]).then_inc(s_repc, 1)

            turn(None, 0, 1)
            with act_e.Fori(0, B // 2 - 1) as i:
                turn(2 * i, 2 * i + 1, 0)
                turn(2 * i + 1, 2 * i + 2, 1)
            turn(B - 2, B - 1, 0)
            turn(B - 1, None, 1)
            phase_end(act_e, 0)
            if upto < 1:
                return

            act_e.wait_ge(s_weights0, 16 * len(WEIGHTS0))
            for b in range(B):
                act_e.wait_ge(s_byt, b + 1)
                nc.scalar.activation(yT_all[:, b * T:(b + 1) * T], bank[:, 2 + b % 2, :], ACT.Copy).then_inc(s_bytc, 1)
            act_e.wait_ge(s_logc, 1)
            nc.scalar.activation(score[:, :, :], score[:, :, :], ACT.Exp).then_inc(s_escore, 1)

            def shared(b0, b1):
                with act_e.Fori(b0, b1) as b:
                    for n in range(SHT):
                        act_e.wait_ge(s_gu, SHT * b + n + 1)
                        if n >= 2:
                            act_e.wait_ge(s_actv, SHT * b + n - 1)
                        nc.scalar.activation(gated[:, n % 2, :], bank[:, 2 + 2 * (n % 2), :],
                                             ACT.Silu).then_inc(s_silu, 1)

            def tiles(i):
                for m in range(8):
                    n = 8 * i + m
                    act_e.wait_ge(s_eup, n + 1)
                    wait(act_e, s_eact, n - 1)
                    nc.scalar.activation(gated[:, m % 2, 0:HID], bank[:, 2 + 2 * (m % 2), 0:HID],
                                         ACT.Silu).then_inc(s_esilu, 1)
                    copy_turned(n, m)

            def copy_turned(n, m):
                act_e.wait_ge(s_tr, n + 3)
                first = isinstance(n, int) and n < 1
                last = isinstance(n, int) and n + 2 >= XT
                k0, k1 = (HT if first else 0), (HT if last else HT + 1)
                nc.scalar.activation(turned[:, m % 4, k0:k1, :].rearrange("p k n -> p (k n)"),
                                     bank[:, 6 + m % 2, k0 * P:k1 * P], ACT.Copy).then_inc(s_trc, 1)

            shared(0, B // 2)
            act_e.wait_ge(s_actv, SHT * B // 2)
            copy_turned(-2, -2)
            copy_turned(-1, -1)
            turns(act_e, XT // 8, tiles, last=True)
            copy_turned(XT, XT)
            act_e.wait_ge(s_eact, XT)
            shared(B // 2, B)
            phase_end(act_e, 1)
            if upto < 2:
                return

            act_e.wait_ge(s_weights1, 16 * len(WEIGHTS1))
            nc.scalar.activation(keep_mu[:, :], vec1[:, 0:4], ACT.Sigmoid).then_inc(s_mu, 1)

            def turn(b, bx, par):
                for e in range(DK):
                    if b is not None:
                        act_e.wait_ge(s_vb, DK * b + e + 1)
                        wait(act_e, s_kv, DK * b + e - 1)
                        nc.scalar.activation(v_all[:, e % 2, :], bank[:, 1 + e % 2, :], ACT.Copy).then_inc(s_vbc, 1)
                    if bx is not None and e in READY:
                        READY[e](bx, 1 - par)

            def neighbours(b, par):
                act_e.wait_ge(s_cyt, b + 1)
                nc.scalar.activation(yT[:, :], bank[:, 6, :], ACT.Copy).then_inc(s_cytc, 1)
                act_e.wait_ge(s_cytc, b + 1)
                for s, shift in enumerate((0, 1, -1, 2)):
                    r = slice(32 * s, 32 * s + 32)
                    for o, i, n in ((max(shift, 0), max(-shift, 0), T - abs(shift)),
                                    (0 if shift > 0 else T + shift, T - shift if shift > 0 else 0, abs(shift))):
                        if n:
                            last = nc.scalar.activation(x_star[r, o:o + n], yT[r, i:i + n], ACT.Copy)
                last.then_inc(s_star, 1)

            def decay_and_k(b, par):
                act_e.wait_ge(s_proj, 5 * b + 1)
                nc.scalar.activation(decay[:, par, :], bank[:, 5, :], ACT.Tanh, scale=vec1[:, 4:5]).then_inc(s_w, 1)
                act_e.wait_ge(s_proj, 5 * b + 2)
                nc.scalar.activation(part1[:, par, 0, :], bank[:, 6, :], ACT.Copy).then_inc(s_hi, 1)
                nc.scalar.activation(k1[:, par, :], bank[:, 6, :], ACT.Copy).then_inc(s_hi, 1)

            def decay_of(b, par):
                act_e.wait_ge(s_w, 3 * b + 1)
                nc.scalar.activation(decay[:, par, :], decay[:, par, :], ACT.Exp, scale=vec1[:, 5:6],
                                     bias=vec1[:, 6:7]).then_inc(s_w, 1)
                act_e.wait_ge(s_w, 3 * b + 2)
                nc.scalar.activation(decay[:, par, :], decay[:, par, :], ACT.Exp, scale=-1.0).then_inc(s_w, 1)

            def gate_r(b, par):
                act_e.wait_ge(s_proj, 5 * b + 3)
                nc.scalar.activation(sig_r[:, par, :], bank[:, 5, :], ACT.Sigmoid).then_inc(s_sig, 1)

            def v_high(b, par):
                act_e.wait_ge(s_proj, 5 * b + 4)
                nc.scalar.activation(part1[:, par, 2, :], bank[:, 0, :], ACT.Copy).then_inc(s_hi, 1)

            def gate_g(b, par):
                act_e.wait_ge(s_proj, 5 * b + 5)
                nc.scalar.activation(sig_g[:, par, :], bank[:, 6, :], ACT.Sigmoid).then_inc(s_sig, 1)

            READY = {4: neighbours, 8: decay_and_k, 9: decay_of, 11: gate_r, 12: v_high, 13: gate_g}
            turn(None, 0, 1)
            turn(0, 1, 0)
            with act_e.Fori(0, B // 2 - 1) as i:
                turn(2 * i + 1, 2 * i + 2, 1)
                turn(2 * i + 2, 2 * i + 3, 0)
            turn(B - 1, None, 1)
            phase_end(act_e, 2)
            if upto < 3:
                return

            def logits_out(b):
                act_e.wait_ge(s_dl, b + 1)
                nc.scalar.activation(lg[:, b * T:(b + 1) * T], bank[0:NE, 2 + b % 2, :], ACT.Copy).then_inc(s_dlc, 1)

            for b in range(B):
                act_e.wait_ge(s_dyt, b + 1)
                if b >= 2:
                    act_e.wait_ge(s_dl, b - 1)
                nc.scalar.activation(pickedT[:, b % 2, :], bank[:, b % 2, :], ACT.Copy).then_inc(s_dytc, 1)
                if b:
                    logits_out(b - 1)
            logits_out(B - 1)
            phase_end(act_e, 3)
            act_e.wait_ge(s_top, 1)
            nc.scalar.activation(prob[:, :], prob[:, :], ACT.Exp, bias=neg_top[:, :],
                                 accum_out=part_sum[:, :]).then_inc(s_pexp, 1)
            phase_end(act_e, 4)

            def experts(i):
                for m in range(4):
                    n, x = 4 * i + m, m // 2
                    act_e.wait_ge(s_xt, n + 1)
                    nc.scalar.activation(pickedT[:, m % 2, :], bank[:, m % 2, :], ACT.Copy).then_inc(s_xtc, 1)
                    for k in range(FT):
                        act_e.wait_ge(s_up, FT * n + k + 1)
                        act_e.nop().then_inc(s_apart_act, 1)
                        nc.scalar.activation(act[:, FT * (m % 2) + k, :], bank[:, 2 + k, :], ACT.Gelu,
                                             bias=fb1[:, ds(i * 2 * FT + x * FT + k, 1)]).then_inc(s_gelu, 1)

            turns(act_e, NE // 2, experts)
            phase_end(act_e, 5)

        @block.vector
        def _(dve):
            ch = Chain(dve, s_dve)
            v = nc.vector
            dve.wait_ge(*consts_in)
            v.tensor_copy(ident_r[:, :], ident[:, :]).then_inc(s_setup, 1)
            v.tensor_copy(spread[:, :, :], spread_f[:, :, :]).then_inc(s_setup, 1)
            v.memset(ones_row[:, :], 1.0).then_inc(s_setup, 1)
            v.memset(max_cols[:, :, :, :].bitcast(fp32), 0.0).then_inc(s_setup, 1)
            ch.link(v.memset(v_tok[:, :, :, :], 0.0))
            v.memset(v_tok[:, :, :, :].rearrange("p a q (h c) -> p (a q h) c", c=32)[:, :, DK:DK + 1],
                     1.0).then_inc(s_setup, 1)
            def embedded(b):
                tiles_b = range(TQ * b, TQ * (b + 1))
                hb = h[:, TQ * b:TQ * (b + 1), :]
                dve.wait_ge(s_emb[b], 16 * TQ)
                ch.link(v.tensor_tensor(hb, hb, tok_b[:, None, :].broadcast_to([P, TQ, D]), ALU.add))
                for j in tiles_b:
                    last = v.bn_stats(stats[:, j, :], h[:, j, :])
                ch.link(last)
                for j in tiles_b:
                    last = v.bn_aggr(mv[:, j, :], stats[:, j, :])
                ch.link(last)
                c = slice(TQ * b, TQ * (b + 1))
                v.tensor_scalar(var_eps[:, c], mv[:, c, 1], EPS, None, ALU.add).then_inc(s_var, 1)

            def inner_variance(b):
                c = slice(TQ * b, TQ * (b + 1))
                dve.wait_ge(s_rstd, b + 1)
                ch.link(v.tensor_tensor(var_eps[:, c], rstd[:, c], rstd[:, c], ALU.mult))
                ch.link(v.tensor_tensor(var_eps[:, c], var_eps[:, c], mv[:, c, 1], ALU.mult))
                v.tensor_scalar(var_eps[:, c], var_eps[:, c], EPS, None, ALU.add).then_inc(s_var2, 1)

            def both_norms(b):
                c = slice(TQ * b, TQ * (b + 1))
                dve.wait_ge(s_rstd2, b + 1)
                ch.link(v.tensor_tensor(rstd[:, c], rstd[:, c], rstd2[:, c], ALU.mult))

            def turn(by, bx, par):
                def ready(f, *a):
                    if bx is not None:
                        f(bx, *a)

                def finish(f):
                    if by is not None:
                        f(by)

                ready(heads_in, 1 - par)
                ready(maxes, range(0, 16))
                ready(max_parts, 0)
                ready(maxes, range(16, 18))
                ready(add_max_rows, 1 - par, 0)
                ready(maxes, range(18, 20))
                ready(add_max_rows, 1 - par, 1)
                ready(maxes, range(20, 24))
                finish(reciprocals)
                ready(maxes, range(24, 28))
                finish(divide)
                ready(maxes, range(28, 32))
                ready(max_parts, 1)
                ready(add_max_rows, 1 - par, 2)
                finish(add_output)
                ready(add_max_rows, 1 - par, 3)

            def heads_in(b, par):
                for j in range(TQ):
                    last = v.tensor_scalar(y[:, j, :], h[:, ds(b * TQ + j, 1), :].rearrange("p a d -> p (a d)"),
                                           mv[:, ds(b * TQ + j, 1), 0], rstd[:, ds(b * TQ + j, 1)],
                                           ALU.subtract, ALU.mult)
                last.then_inc(s_y, 1)
                dve.wait_ge(s_qkv, 3 * b + 1)
                ch.link(v.tensor_scalar(part[:, 0, :], bank[:, 2, :], vec[:, 2:3], None, ALU.add))
                v.scalar_tensor_tensor(part[:, 1, :], bank[:, 2, :], vec[:, 2:3], part[:, 0, :].bitcast(fp32),
                                       ALU.add, ALU.subtract).then_inc(s_split, 1)
                dve.wait_ge(s_qkv, 3 * b + 2)
                ch.link(v.scalar_tensor_tensor(k_full[:, :], bank[:, 3, :], vec[:, 3:4], pe[:, :],
                                               ALU.add, ALU.add))
                ch.link(v.tensor_copy(part[:, 2, :], k_full[:, :]))
                v.tensor_tensor(part[:, 3, :], k_full[:, :], part[:, 2, :].bitcast(fp32),
                                ALU.subtract).then_inc(s_split, 1)
                dve.wait_ge(s_qkv, 3 * b + 3)
                v.tensor_tensor(v_tok[:, par, :, :].rearrange("p q (h c) -> p q h c", c=32)[:, :, :, 0:DK],
                                bank[:, 0, :].rearrange("p (q h d) -> p q h d", q=TQ, h=NH),
                                bv[:, :].rearrange("p (h d) -> p h d", h=NH)[:, None, :, :]
                                .broadcast_to([P, TQ, NH, DK]), ALU.add).then_inc(s_v, 1)

            def maxes(b, units):
                for m in units:
                    h4, qt = (m % NQ) // TQ, m % TQ
                    dve.wait_ge(s_s1, NU1 * b + m + 1)
                    v.tensor_reduce(neg_max[:, m // NQ, qt, h4:h4 + 1], bank[:, 2 + m % 2, :], AX, ALU.max,
                                    negate=True).then_inc(s_max, 1)

            def max_parts(b, g):
                dve.wait_ge(s_max, NU1 * b + NQ * (g + 1))
                hi = [max_cols[:, 2 * g + pp, :, :].rearrange("p q (a c) -> p q a c", a=2)[:, :, :, 3 * DK]
                      for pp in range(2)]
                lo = [max_cols[:, 2 * g + pp, :, :].rearrange("p q (a c) -> p q a c", a=2)[:, :, :, 3 * DK + 1]
                      for pp in range(2)]
                for pp in range(2):
                    last = v.tensor_copy(hi[pp], neg_max[:, g, :, 2 * pp:2 * pp + 2])
                ch.link(last)
                for pp in range(2):
                    last = v.tensor_tensor(lo[pp], neg_max[:, g, :, 2 * pp:2 * pp + 2], hi[pp].bitcast(fp32),
                                           ALU.subtract)
                last.then_inc(s_m, 1)

            def add_max_rows(b, par, p):
                dve.wait_ge(s_mrow, 4 * b + p + 1)
                v.tensor_tensor(qm_rows[:, par, p, :], q_rows[:, p, :].bitcast(fp32), bank[:, 0, :],
                                ALU.add).then_inc(s_qm, 1)

            def reciprocals(b):
                dve.wait_ge(s_sum, b + 1)
                ch.link(v.reciprocal(recip[:, :], bank[:, 1, 0:NG * TQ * GH]))
                v.tensor_copy(recip_cols[:, :, :, :].rearrange("p g q (a c) -> p (g q a) c", a=GH),
                              recip[:, :, None].broadcast_to([P, NG * TQ * GH, 32])).then_inc(s_rec, 1)

            def divide(b):
                for g in range(NG):
                    dve.wait_ge(s_bc, 2 * b + g + 1)
                    v.tensor_tensor(ctx_n[:, g, :], ctx_raw[:, g, :], bank[:, 1 - g, :], ALU.mult).then_inc(s_cn, 1)

            def add_output(b):
                dve.wait_ge(s_o, b + 1)
                hb = h[:, ds(b * TQ, TQ), :]
                ch.link(v.tensor_tensor(hb, hb, bank[:, 1, :].rearrange("p (q d) -> p q d", q=TQ), ALU.add))

            embedded(0)
            inner_variance(0)
            both_norms(0)
            turn(None, 0, 1)
            for stage in (embedded, inner_variance, both_norms):
                for b in range(1, B):
                    stage(b)
            with dve.Fori(0, B // 2 - 1) as i:
                ch.enter(i, 2 * (5 + 2))
                turn(2 * i, 2 * i + 1, 0)
                turn(2 * i + 1, 2 * i + 2, 1)
            ch.leave(B // 2 - 1)
            turn(B - 2, B - 1, 0)
            turn(B - 1, None, 1)
            phase_end(dve, 0)
            if upto < 1:
                return

            dve.wait_ge(s_weights0, 16 * len(WEIGHTS0))
            dve.wait_ge(s_routing, 16 * len(ROUTING))

            def row(a, j):
                return a[:, ds(j, 1), :].rearrange("p a d -> p (a d)")

            def statistics(b, signal):
                for j in range(b * TQ, (b + 1) * TQ):
                    last = v.bn_stats(stats[:, j, :], h[:, j, :])
                ch.link(last)
                for j in range(b * TQ, (b + 1) * TQ):
                    last = v.bn_aggr(mv[:, j, :], stats[:, j, :])
                ch.link(last)
                c = slice(b * TQ, (b + 1) * TQ)
                v.tensor_scalar(var_eps[:, c], mv[:, c, 1], EPS, None, ALU.add).then_inc(signal, 1)

            def normalise_b(b):
                dve.wait_ge(s_brstd, b + 1)
                for j in range(b * TQ, (b + 1) * TQ):
                    last = v.tensor_scalar(y_all[:, j, :], h[:, j, :], mv[:, j, 0:1], rstd[:, j:j + 1],
                                           ALU.subtract, ALU.mult)
                last.then_inc(s_by, 1)

            for b in range(B):
                statistics(b, s_bvar)
                if b:
                    normalise_b(b - 1)
            normalise_b(B - 1)
            wide = [P, NT, NE]
            dve.wait_ge(s_logit, 1)
            ch.link(v.tensor_copy(logit[:, :, :], bank[:, 1, 0:NT * NE].rearrange("p (j e) -> p j e", e=NE)))
            ch.link(v.tensor_reduce(top[:, :], logit[:, :, :], AX, ALU.max))
            v.tensor_tensor(score[:, :, :], logit[:, :, :], top[:, :, None].broadcast_to(wide),
                            ALU.subtract).then_inc(s_logc, 1)
            dve.wait_ge(s_escore, 1)
            ch.link(v.tensor_reduce(top[:, :], score[:, :, :], AX, ALU.add))
            ch.link(v.reciprocal(top[:, :], top[:, :]))
            ch.link(v.tensor_tensor(score[:, :, :], score[:, :, :], top[:, :, None].broadcast_to(wide), ALU.mult))
            pairs = [P, NT, NE, NE]
            other, own = score[:, :, None, :].broadcast_to(pairs), score[:, :, :, None].broadcast_to(pairs)
            v.tensor_tensor(better[:, :, :, :], other, own, ALU.is_gt)
            ch.link(v.tensor_tensor(tied[:, :, :, :], other, own, ALU.is_equal))
            ch.link(v.tensor_tensor(tied[:, :, :, :], tied[:, :, :, :], tri[:, None, :, :].broadcast_to(pairs),
                                    ALU.mult))
            ch.link(v.tensor_tensor(better[:, :, :, :].rearrange("p q e f -> p (q e f)"),
                                    better[:, :, :, :].rearrange("p q e f -> p (q e f)"),
                                    tied[:, :, :, :].rearrange("p q e f -> p (q e f)"), ALU.add))
            ch.link(v.tensor_reduce(rank_e[:, :, :], better[:, :, :, :], AX, ALU.add))
            v.tensor_scalar(chosen_e[:, :, :].rearrange("p e j -> p j e"), rank_e[:, :, :], float(TOPK), None,
                            ALU.is_lt).then_inc(s_before, 1)
            for k in range(TOPK):
                last = v.tensor_scalar(sel[:, k, :, :], rank_e[:, :, :], float(k), None, ALU.is_equal)
            ch.link(last)
            dve.wait_ge(s_total, 1)
            dve.wait_ge(s_setup, 7)
            flat = "p e j -> p (e j)"
            ch.link(v.tensor_copy(total[:, :, :].rearrange(flat), bank[:, 0, 0:NE * NT]))
            ch.link(v.tensor_reduce(taken[:, :], total[:, :, :], AX, ALU.add))
            ch.link(v.tensor_scalar(taken[:, :], taken[:, :], float(P - 1), None, ALU.add))
            ch.link(v.tensor_copy(taken_i[:, :], taken[:, :]))
            ch.link(v.tensor_scalar(taken_i[:, :], taken_i[:, :], 7, None, ALU.arith_shift_right))
            ch.link(v.tensor_copy(tiles_of[:, :], taken_i[:, :]))
            ch.link(v.tensor_tensor_scan(tile_end[:, :], all_ones[:, 0:NE], tiles_of[:, :], 0.0, ALU.mult, ALU.add))
            v.tensor_tensor(row_base[:, :], tile_end[:, :], tiles_of[:, :], ALU.subtract)
            ch.link(v.tensor_tensor(past[:, :, :], tile_up[:, :, None].broadcast_to([1, XT, NE]),
                                    tile_end[0:1, None, :].broadcast_to([1, XT, NE]), ALU.is_ge))
            ch.link(v.tensor_reduce(owner_f[:, :], past[:, :, :], AX, ALU.add))
            ch.link(v.tensor_scalar(owner_f[:, :], owner_f[:, :], float(NE - 1), None, ALU.min))
            v.tensor_copy(owner[:, :], owner_f[:, :]).then_inc(s_owner, 1)
            ch.link(v.tensor_tensor_scan(upto_tile[:, :, :].rearrange(flat), goes_on[:, :, :].rearrange(flat),
                                         total[:, :, :].rearrange(flat), 0.0, ALU.mult, ALU.add))
            ch.link(v.tensor_tensor(upto_tile[:, :, :], upto_tile[:, :, :], total[:, :, :], ALU.subtract))
            ch.link(v.tensor_tensor(place_e[:, :, :].rearrange(flat), upto_tile[:, :, :].rearrange(flat),
                                    bank[:, 7, 0:NE * NT], ALU.add))
            ch.link(v.scalar_tensor_tensor(place_e[:, :, :], row_base[:, :, None].broadcast_to([P, NE, NT]),
                                           float(P), place_e[:, :, :], ALU.mult, ALU.add))
            for k in range(TOPK):
                last = v.tensor_tensor(picked_e[:, k, :, :], sel[:, k, :, :],
                                       place_e[:, :, :].rearrange("p e j -> p j e"), ALU.mult)
            ch.link(last)
            for k in range(TOPK):
                last = v.tensor_reduce(row_f[:, k, :], picked_e[:, k, :, :], AX, ALU.add)
            ch.link(last)
            v.tensor_copy(row_id[:, :, :], row_f[:, :, :]).then_inc(s_rows, 1)
            for k in range(TOPK):
                last = v.tensor_tensor(picked_e[:, k, :, :], sel[:, k, :, :], score[:, :, :], ALU.mult)
            ch.link(last)
            for k in range(TOPK):
                last = v.tensor_reduce(weight[:, k, :], picked_e[:, k, :, :], AX, ALU.add)
            ch.link(last)

            def shared(b):
                for n in range(SHT):
                    dve.wait_ge(s_silu, SHT * b + n + 1)
                    v.tensor_tensor(act[:, n, :], gated[:, n % 2, :], bank[:, 3 + 2 * (n % 2), :],
                                    ALU.mult).then_inc(s_actv, 1)
                dve.wait_ge(s_ye, b + 1)
                hb = h[:, ds(b * TQ, TQ), :].rearrange("p q d -> p (q d)")
                dve.nop().then_inc(s_apart, 1)
                ch.step(v.tensor_tensor(hb, bank[:, 6, :], hb, ALU.add))
                ch.wait()
                dve.nop().then_inc(s_yec, 1)

            def tiles(i):
                for m in range(8):
                    n = 8 * i + m
                    if m == 2 and not (isinstance(i, int) and i == 0):
                        rows_out(i, -1)
                    if m == 6:
                        rows_out(i, 0)
                    dve.wait_ge(s_esilu, n + 1)
                    dve.wait_ge(s_tr, n + 2)
                    v.tensor_tensor(act[:, SHT + m % 2, 0:HID], gated[:, m % 2, 0:HID],
                                    bank[:, 3 + 2 * (m % 2), 0:HID], ALU.mult).then_inc(s_eact, 1)

            def rows_out(i, k):
                par = k % 2
                dve.wait_ge(s_edown, TQ * (2 * i + k + 1))
                wait(dve, s_estore[par], 16 * i)
                v.tensor_copy(e_rows[:, par, :, :].rearrange("p q d -> p (q d)"), bank[:, par, :]).then_inc(s_erows, 1)

            dve.nop().then_inc(s_estore[1], 16)
            dve.wait_ge(s_cleared, 16)
            ch.enter(0, 1)
            start1 = ch.start
            with dve.Fori(0, B // 2) as b:
                ch.base, ch.n = start1 + b, 0
                shared(b)
            turns(dve, XT // 8, tiles)
            rows_out(XT // 8, -1)
            base1 = start1 + B // 2
            with dve.Fori(0, B // 2) as i:
                ch.base, ch.n = base1 + 5 * i, 0
                shared(B // 2 + i)
                for par in range(2):
                    b = 2 * i + par
                    dve.wait_ge(s_back[par], 16 * TQ * TOPK * (i + 1))
                    dve.nop().then_inc(s_apart, 1)
                    for k in range(TOPK):
                        for q in range(TQ):
                            last = v.scalar_tensor_tensor(row(h, b * TQ + q), back[:, par, q, k, :],
                                                          weight[:, k, ds(b * TQ + q, 1)], row(h, b * TQ + q),
                                                          ALU.mult, ALU.add)
                        ch.link(last, apart=s_apart)
                    dve.nop().then_inc(s_added, 1)
            ch.base, ch.n = base1 + 5 * (B // 2), 0
            phase_end(dve, 1)
            if upto < 2:
                return

            dve.wait_ge(s_weights1, 16 * len(WEIGHTS1))
            dve.wait_ge(s_mu, 1)
            v.tensor_scalar(keep_mu[:, :], keep_mu[:, :], -1.0, 1.0, ALU.mult, ALU.add).then_inc(s_setup, 1)
            v.tensor_copy(pick[:, :, :].rearrange("p e n -> p (e n)"), pick_f).then_inc(s_setup, 1)
            v.tensor_copy(head_ones_r[:, :], head_ones[:, :]).then_inc(s_setup, 1)
            v.memset(fwd[:, :, 0:1], 0.0).then_inc(s_setup, 1)
            v.memset(bwd[:, :, T:T + 1], 0.0).then_inc(s_setup, 1)
            dve.wait_ge(s_setup, 12)
            def turn(b, bx, bg, par):
                for e in range(DK):
                    if b is not None:
                        scans(b, par, e)
                        if e:
                            terms(b, e - 1)
                        elif bg is not None:
                            terms(bg, DK - 1)
                    if bg is not None and e in FINISH:
                        FINISH[e](bg, 1 - par)
                    if bx is not None and e in READY:
                        READY[e](bx, 1 - par)

            def scans(b, par, e):
                if e == 0:
                    dve.wait_ge(s_w, 3 * b + 3)
                dve.wait_ge(s_kv, DK * b + e + 1)
                wait(dve, s_both, DK * b + e - 1)
                v.tensor_tensor_scan(fwd[:, e % 2, 1:T + 1], decay[:, par, :], kv[:, e % 2, :], 0.0,
                                     ALU.mult, ALU.add)
                v.tensor_tensor_scan(bwd[:, e % 2, 0:T][:, ::-1], decay[:, par, ::-1], kv[:, e % 2, ::-1], 0.0,
                                     ALU.mult, ALU.add).then_inc(s_scan, 1)

            def terms(b, e):
                dve.wait_ge(s_both, DK * b + e + 1)
                dve.wait_ge(s_kb, DK * b + e + 1)
                wait(dve, s_acc, DK * b + e - 1)
                v.tensor_tensor(term[:, e % 2, :], both[:, e % 2, :], bank[:, 3 + e % 2, :],
                                ALU.mult).then_inc(s_term, 1)

            def output_stats(b, par):
                dve.wait_ge(s_acc, DK * b + DK)
                ch.link(v.scalar_tensor_tensor(wkv[:, :], bank[:, 7, :], 0.5, bonus[:, par, :], ALU.mult, ALU.add))
                dve.nop().then_inc(s_wkv, 1)
                dve.wait_ge(s_sig, 2 * b + 1)
                ch.link(v.tensor_tensor(wkv[:, :], wkv[:, :], sig_r[:, par, :], ALU.mult))
                ch.link(v.bn_stats(gn_stat[:, :], wkv[:, :]), apart=s_apart)
                v.bn_aggr(gn_mv[:, :], gn_stat[:, :]).then_inc(s_gm, 1)

            def group_mean(b, par):
                dve.wait_ge(s_gmr, 2 * b + 1)
                dve.wait_ge(s_gm, 2 * b + 1)
                ch.link(v.tensor_scalar(gn_mean[:, :], bank[:, 0, 0:1], 1.0 / DK, None, ALU.mult))
                ch.link(v.tensor_tensor(gn_dev[:, :], gn_mv[:, 0:1], gn_mean[:, :], ALU.subtract))
                ch.link(v.tensor_tensor(gn_dev[:, :], gn_dev[:, :], gn_dev[:, :], ALU.mult))
                v.tensor_tensor(gn_dev[:, :], gn_dev[:, :], gn_mv[:, 1:2], ALU.add).then_inc(s_gm, 1)

            def group_variance(b, par):
                dve.wait_ge(s_gmr, 2 * b + 2)
                v.tensor_scalar(gn_var[:, :], bank[:, 0, 2:3], 1.0 / DK, EPS, ALU.mult, ALU.add).then_inc(s_gvar, 1)

            def group_norm(b, par):
                dve.wait_ge(s_grstd, b + 1)
                ch.link(v.tensor_tensor(gn_gain[:, :], gn_rstd[:, :], vec1[:, 8:9], ALU.mult))
                ch.link(v.tensor_tensor(gn_off[:, :], gn_gain[:, :], gn_mean[:, :], ALU.mult))
                ch.link(v.tensor_tensor(gn_off[:, :], vec1[:, 9:10], gn_off[:, :], ALU.subtract))
                dve.wait_ge(s_sig, 2 * b + 2)
                ch.link(v.tensor_scalar(wkv[:, :], wkv[:, :], gn_gain[:, :], gn_off[:, :], ALU.mult, ALU.add))
                v.tensor_tensor(wkv[:, :], wkv[:, :], sig_g[:, par, :], ALU.mult).then_inc(s_on, 1)

            def add_output(b, par):
                dve.wait_ge(s_co, b + 1)
                hb = h[:, ds(b * TQ, TQ), :]
                ch.link(v.tensor_tensor(hb, hb, bank[:, 0, :].rearrange("p (q d) -> p q d", q=TQ), ALU.add))

            def token_stats(b, par):
                for q in range(TQ):
                    last = v.bn_stats(stats[:, q, :], row(h, b * TQ + q))
                ch.link(last, apart=s_apart)
                for q in range(TQ):
                    last = v.bn_aggr(mv[:, q, :], stats[:, q, :])
                ch.link(last)
                v.tensor_scalar(var_eps[:, 0:TQ], mv[:, 0:TQ, 1], EPS, None, ALU.add).then_inc(s_cvar, 1)

            def normalise(b, par):
                dve.wait_ge(s_crstd, b + 1)
                dve.nop().then_inc(s_apart, 1)
                for q in range(TQ):
                    last = v.tensor_scalar(y[:, q, :], row(h, b * TQ + q), mv[:, q, 0:1], rstd[:, q:q + 1],
                                           ALU.subtract, ALU.mult)
                last.then_inc(s_cy, 1)

            def mix(*inputs):
                def part_of(b, par):
                    dve.wait_ge(s_star, b + 1)
                    for m in inputs:
                        v.scalar_tensor_tensor(mixed[:, m, :], x_star[:, :], keep_mu[:, m:m + 1], yT[:, :],
                                               ALU.mult, ALU.add).then_inc(s_mix, 1)
                return part_of

            def low_part(n, bk, hi):
                def part_of(b, par):
                    dve.wait_ge(s_hi, 3 * b + hi)
                    v.tensor_tensor(part1[:, par, 2 * n + 1, :], bank[:, bk, :], part1[:, par, 2 * n, :].bitcast(fp32),
                                    ALU.subtract).then_inc(s_lo, 1)
                return part_of

            def bonus_of(b, par):
                dve.wait_ge(s_vsum, b + 1)
                ch.link(v.scalar_tensor_tensor(bonus[:, par, :], k1[:, par, :], vec1[:, 7:8], bank[:, 0, :],
                                               ALU.mult, ALU.mult))

            FINISH = {1: output_stats, 4: group_mean, 6: group_variance, 8: group_norm, 10: add_output}
            READY = {0: token_stats, 2: normalise, 5: mix(3, 1), 6: mix(0), 9: low_part(0, 6, 2), 10: mix(2),
                     13: low_part(1, 0, 3), 15: bonus_of}
            turn(None, 0, None, 1)
            turn(0, 1, None, 0)
            with dve.Fori(0, B // 2 - 1) as i:
                ch.enter(i, 2 * (11 + 3))
                turn(2 * i + 1, 2 * i + 2, 2 * i, 1)
                turn(2 * i + 2, 2 * i + 3, 2 * i + 1, 0)
            ch.leave(B // 2 - 1)
            turn(B - 1, None, B - 2, 1)
            terms(B - 1, DK - 1)
            for e in FINISH:
                FINISH[e](B - 1, 1)
            phase_end(dve, 2)
            if upto < 3:
                return

            v.memset(zeros[:, :], 0.0).then_inc(s_zero, 1)
            v.memset(ones_cw[:, :], 1.0).then_inc(s_setup, 1)
            v.memset(thr[:, :], 0).then_inc(s_setup, 1)

            def normalise_d(b):
                dve.wait_ge(s_drstd, b + 1)
                if b >= 2:
                    dve.wait_ge(s_dyt, b - 1)
                    dve.wait_ge(s_ystore[b % 2], 16 * (b // 2))
                for q in range(TQ):
                    j = b * TQ + q
                    last = v.tensor_scalar(picked[:, b % 2, q, :], h[:, j, :], mv[:, j, 0:1], rstd[:, j:j + 1],
                                           ALU.subtract, ALU.mult)
                last.then_inc(s_dy, 1)

            for b in range(B):
                statistics(b, s_dvar)
                if b:
                    normalise_d(b - 1)
            normalise_d(B - 1)
            phase_end(dve, 3)
            dve.wait_ge(s_spread, 16)
            v.tensor_reduce(part_top[:, :], prob[:, :], AX, ALU.max).then_inc(s_ptop, 1)
            dve.wait_ge(s_ptopt, 1)
            ch.link(v.tensor_reduce(expert_top[:, :], bank[0:1, 4, 0:P].rearrange("p (e c) -> p e c", e=NE), AX,
                                    ALU.max, negate=True))
            v.tensor_copy(top_row[:, :, :], expert_top[:, :, None].broadcast_to([1, NE, NC])).then_inc(s_etop, 1)
            dve.wait_ge(s_ebias, 1)
            v.tensor_copy(neg_top[:, :], bank[:, 5, 0:1]).then_inc(s_top, 1)
            dve.wait_ge(s_psum, 1)
            ch.link(v.reciprocal(rsum[:, :], bank[:, 6, 0:1]))
            dve.wait_ge(s_pexp, 1)
            ch.link(v.tensor_scalar(prob[:, :], prob[:, :], rsum[:, :], None, ALU.mult))
            dve.wait_ge(s_weights2, 16 * len(WEIGHTS2))
            dve.wait_ge(s_setup, 14)
            with dve.Fori(0, 30) as i:
                ch.enter(i, 3)
                ch.link(v.tensor_tensor(cand[:, :], thr[:, :], bits[:, ds(i, 1)], ALU.bitwise_or))
                v.tensor_scalar(hit[:, :], prob[:, :], cand[:, :].bitcast(fp32), None, ALU.is_ge, ALU.add,
                                accum_out=count[:, :]).then_inc(s_cnt, 1)
                dve.wait_ge(s_tot, i + 1)
                dve.wait_ge(s_cnt, i + 1)
                ch.link(v.tensor_scalar(keep[:, :], bank[:, 0, 0:1], float(CAP), None, ALU.is_ge), apart=s_apart)
                ch.link(v.copy_predicated(thr[:, :], keep[:, :], cand[:, :]))
            ch.leave(30)
            thr_f = thr[:, :].bitcast(fp32)
            ch.step(v.tensor_scalar(chosen[:, :], prob[:, :], thr_f, None, ALU.is_gt, ALU.add,
                                    accum_out=count[:, :]))
            ch.wait()
            dve.nop().then_inc(s_cnt, 1)
            dve.wait_ge(s_tot, 31)
            ch.link(v.tensor_scalar(need[:, :], bank[:, 0, 1:2], -1.0, float(CAP), ALU.mult, ALU.add))
            ch.link(v.tensor_scalar(hit[:, :], prob[:, :], thr_f, None, ALU.is_equal))
            ch.link(v.tensor_tensor_scan(rank[:, :], ones_cw[:, :], hit[:, :], 0.0, ALU.mult, ALU.add))
            v.tensor_copy(count[:, :], rank[:, CW - 1:CW]).then_inc(s_cnt, 1)
            dve.wait_ge(s_tot, 32)
            ch.link(v.tensor_tensor(rank[:, :], rank[:, :], hit[:, :], ALU.subtract))
            ch.link(v.tensor_scalar(rank[:, :], rank[:, :], bank[:, 0, 2:3], need[:, :], ALU.add, ALU.is_lt))
            ch.link(v.tensor_tensor(hit[:, :], hit[:, :], rank[:, :], ALU.mult))
            ch.link(v.tensor_tensor(chosen[:, :], chosen[:, :], hit[:, :], ALU.add))
            ch.link(v.tensor_tensor_scan(slot[:, :], ones_cw[:, :], chosen[:, :], 0.0, ALU.mult, ALU.add))
            v.tensor_copy(count[:, :], slot[:, CW - 1:CW]).then_inc(s_cnt, 1)
            dve.wait_ge(s_tot, 33)
            ch.link(v.scalar_tensor_tensor(slot[:, :], slot[:, :], bank[:, 0, 3:4], chosen[:, :],
                                           ALU.add, ALU.mult))
            v.tensor_scalar(slot[:, :], slot[:, :], -1.0, None, ALU.add).then_inc(s_slots, 1)
            dve.wait_ge(s_slotst, 1)
            v.tensor_copy(slot_i[:, :], bank[:, 1, 0:2 * P])
            ch.link(v.tensor_copy(comb1[:, :], bank[:, 1, 2 * P:4 * P]))
            v.tensor_scalar(low_i[:, :], slot_i[:, :], P - 1, None, ALU.bitwise_and)
            ch.link(v.tensor_scalar(slot_i[:, :], slot_i[:, :], 7, None, ALU.arith_shift_right))
            v.tensor_copy(slot_lo[:, :], low_i[:, :])
            ch.step(v.tensor_copy(slot_hi[:, :], slot_i[:, :]))
            ch.link(v.tensor_copy(w_a[:, :], comb1[:, :]))
            ch.link(v.tensor_tensor(w_rest[:, :], comb1[:, :], w_a[:, :], ALU.subtract))
            ch.link(v.tensor_copy(w_b[:, :], w_rest[:, :]))
            ch.link(v.tensor_tensor(w_c[:, :], w_rest[:, :], w_b[:, :], ALU.subtract))
            wide = [P, 2 * P, SH]
            ch.link(v.tensor_tensor(in_hi[:, :, :], slot_hi[:, :, None].broadcast_to(wide),
                                    count_up[:, None, 0:SH].broadcast_to(wide), ALU.is_equal))
            v.tensor_scalar(entry[:, :, 0, :], in_hi[:, :, :], row_no[:, :], None, ALU.mult)
            for n, a in enumerate((tile_no, w_a, w_b, w_c)):
                last = v.tensor_tensor(entry[:, :, 1 + n, :], in_hi[:, :, :], a[:, :, None].broadcast_to(wide),
                                       ALU.mult)
            last.then_inc(s_entry, 1)

            by_chunk = slot_lo[:, :].rearrange("p (k c) -> p k c", c=NC)

            def one_hots(c, par):
                wait(dve, s_hotc, 2 * NE * (c - 1))
                v.tensor_tensor(onehot[:, par, :, :], by_chunk[:, :, ds(c, 1)].broadcast_to([P, 2 * NE, P]),
                                count_up[:, None, :].broadcast_to([P, 2 * NE, P]),
                                ALU.is_equal).then_inc(s_hot, 1)

            def two_chunks(i):
                for par in range(2):
                    one_hots(2 * i + par, par)

            turns(dve, NC // 2, two_chunks)
            dve.wait_ge(s_hotc, 2 * NE * NC)
            ch.link(v.tensor_copy(list_raw[:, :, :, :].rearrange("p e a s -> p (e a s)"),
                                  bank[:, 2, 0:NE * 5 * SH]))
            ch.link(v.scalar_tensor_tensor(list_f[:, :, :], list_raw[:, :, 1, :], float(P), list_raw[:, :, 0, :],
                                           ALU.mult, ALU.add))
            ch.step(v.tensor_copy(list_id[:, :].rearrange("p (e s) -> p e s", e=NE), list_f[:, :, :]))
            ch.link(v.tensor_tensor(list_w[:, :, :], list_raw[:, :, 2, :], list_raw[:, :, 3, :], ALU.add))
            ch.link(v.tensor_tensor(list_w[:, :, :], list_w[:, :, :], list_raw[:, :, 4, :], ALU.add))
            dve.nop().then_inc(s_lists, 1)
            phase_end(dve, 4)
            lw = list_w[:, :, :].rearrange("p e s -> p (e s)")

            def experts(i):
                for m in range(4):
                    n = 4 * i + m
                    dve.wait_ge(s_fo, n + 1)
                    wait(dve, s_scatter[m % 2], 16 * TQ * (2 * i + m // 2))
                    for q in range(TQ):
                        last = v.tensor_scalar(out_rows[:, m % 2, q, :], bank[:, 6 + m % 2, q * P:(q + 1) * P],
                                               lw[:, ds(n * TQ + q, 1)], None, ALU.mult)
                    last.then_inc(s_wy, 1)

            turns(dve, NE // 2, experts)
            phase_end(dve, 5)

        @block.tensor
        def _(te):
            te.wait_ge(*consts_in)
            te.wait_ge(s_setup, 5)
            mm = te.matmul
            def turn(by, bx, par):
                for u in range(NU2):
                    if by is not None:
                        scores2(by, par, u)
                        if u >= 3 and u % 2:
                            contexts(by, par, (u - 3) // 2)
                    if bx is not None:
                        if u == 0:
                            turn_tokens(bx)
                        elif u == 1:
                            project(bx)
                        elif u < 6:
                            rows_of_heads(bx, u - 2)
                        else:
                            if u == 15:
                                max_rows(bx, None, 0)
                            scores1(bx, 1 - par, range(2 * (u - 6), 2 * (u - 5)))
                if by is not None:
                    contexts(by, par, 7)
                if bx is not None:
                    max_rows(bx, None, 1)
                    scores1(bx, 1 - par, range(20, 24))
                if by is not None:
                    sums(by)
                if bx is not None:
                    scores1(bx, 1 - par, range(24, 28))
                if by is not None:
                    broadcast_recips(by, bx)
                if bx is not None:
                    scores1(bx, 1 - par, range(28, 32))
                    max_rows(bx, by, 2)
                if by is not None:
                    output(by)
                if bx is not None:
                    max_rows(bx, by, 3)

            def turn_tokens(b):
                te.wait_ge(s_y, b + 1)
                wait(te, s_qm, 4 * b)
                for q in range(TQ):
                    last = te.transpose(bank[:, 0, q * P:(q + 1) * P], y[:, q, :], ident[:, :])
                last.then_inc(s_yt, 1)

            def project(b):
                te.wait_ge(s_ytc, b + 1)
                wait(te, s_max, NU1 * b)
                mm(bank[:, 2, :], wq[:, :], yT[:, :], start=True, stop=True).then_inc(s_qkv, 1)
                mm(bank[:, 3, :], wk[:, :], yT[:, :], start=True, stop=True).then_inc(s_qkv, 1)
                for q in range(TQ):
                    last = mm(bank[:, 0, q * P:(q + 1) * P], yT[:, q * P:(q + 1) * P], wv[:, :],
                              start=True, stop=True)
                last.then_inc(s_qkv, 1)

            def rows_of_heads(b, p):
                for to_k in range(2):
                    n = 2 * p + to_k
                    te.wait_ge(s_split, 2 * b + 1 + to_k)
                    if n >= 2:
                        te.wait_ge(s_repc, 8 * b + n - 1)
                    for lo in range(2):
                        last = mm(bank[:, 2 + to_k, :], spread[:, 2 * to_k + lo, p * P:(p + 1) * P],
                                  part[:, 2 * to_k + lo, :], start=(lo == 0), stop=(lo == 1))
                    last.then_inc(s_rep, 1)

            def scores1(b, par, units):
                for m in units:
                    g, h4, qt = m // NQ, (m % NQ) // TQ, m % TQ
                    if m == 0:
                        te.wait_ge(s_repc, 8 * b + 8)
                    if m >= 2:
                        te.wait_ge(s_max, NU1 * b + m - 1)
                    p, r = 2 * g + h4 // 2, 64 * (h4 % 2)
                    mm(bank[:, 2 + m % 2, :], q_rows[r:r + 64, p, qt * P:(qt + 1) * P],
                       k_rows[r:r + 64, par, p, :], start=True, stop=True).then_inc(s_s1, 1)

            def max_rows(b, by, p):
                te.wait_ge(s_m, 2 * b + p // 2 + 1)
                if p == 0:
                    te.wait_ge(s_v, b + 1)
                elif p == 2 and by is not None:
                    te.wait_ge(s_cn, 2 * by + 2)
                else:
                    te.wait_ge(s_qm, 4 * b + p)
                for q in range(TQ):
                    last = mm(bank[:, 0, q * P:(q + 1) * P], max_cols[:, p, q, :], ident_r[:, :],
                              start=True, stop=True)
                last.then_inc(s_mrow, 1)

            def scores2(b, par, u):
                g, kt, pp = u // 8, (u % 8) // 2, u % 2
                p = 2 * g + pp
                te.wait_ge(s_qm, 4 * b + p + 1)
                if u >= 2:
                    te.wait_ge(s_exp, NU2 * b + u - 1)
                for hh in range(2):
                    r = 64 * hh
                    last = mm(bank[:, 4 + 2 * (u % 2) + hh, :], k_rows[r:r + 64, par, p, kt * P:(kt + 1) * P],
                              qm_rows[r:r + 64, par, p, :], start=True, stop=True)
                last.then_inc(s_s2, 1)

            def contexts(b, par, a):
                g, kt = a // 4, a % 4
                te.wait_ge(s_exp, NU2 * b + 2 * a + 2)
                if a == 0:
                    te.wait_ge(s_qm, 4 * b + 4)
                elif a == 4:
                    te.wait_ge(s_ctx, 2 * b + g)
                for h4 in range(GH):
                    last = mm(bank[32 * h4:32 * h4 + 32, 1, :],
                              v_tok[:, par, kt, g * P + 32 * h4:g * P + 32 * h4 + 32],
                              probs[:, (2 * a) % 4 + h4 // 2, h4 % 2, :],
                              start=(kt == 0), stop=(kt == TQ - 1), tile_position=(0, 32 * h4))
                last.then_inc(s_av, 1)

            def sums(b):
                te.wait_ge(s_ctx, 2 * b + 2)
                for g in range(NG):
                    for q in range(TQ):
                        last = mm(bank[:, 1, (g * TQ + q) * GH:(g * TQ + q + 1) * GH],
                                  ctx_raw[:, g, q * P:(q + 1) * P], pick_sum[:, :], start=True, stop=True)
                last.then_inc(s_sum, 1)

            def broadcast_recips(b, bx):
                te.wait_ge(s_rec, b + 1)
                if bx is not None:
                    te.wait_ge(s_qm, 4 * bx + 2)
                for g in range(NG):
                    for q in range(TQ):
                        last = mm(bank[:, 1 - g, q * P:(q + 1) * P], recip_cols[:, g, q, :], ident[:, :],
                                  start=True, stop=True)
                    last.then_inc(s_bc, 1)

            def output(b):
                te.wait_ge(s_cn, 2 * b + 2)
                for q in range(TQ):
                    o = bank[:, 1, q * P:(q + 1) * P]
                    for g in range(NG):
                        mm(o, ctx_n[:, g, q * P:(q + 1) * P], wo[:, g, :], start=(g == 0), stop=False)
                    last = mm(o, ones_row[:, 0:P], bo_row[:, :], start=False, stop=True)
                last.then_inc(s_o, 1)

            turn(None, 0, 1)
            with te.Fori(0, B // 2 - 1) as i:
                turn(2 * i, 2 * i + 1, 0)
                turn(2 * i + 1, 2 * i + 2, 1)
            turn(B - 2, B - 1, 0)
            turn(B - 1, None, 1)
            phase_end(te, 0)
            if upto < 1:
                return

            te.wait_ge(s_weights0, 16 * len(WEIGHTS0))
            te.wait_ge(s_routing, 16 * len(ROUTING))
            for b in range(B):
                te.wait_ge(s_by, b + 1)
                if b >= 2:
                    te.wait_ge(s_bytc, b - 1)
                for q in range(TQ):
                    last = te.transpose(bank[:, 2 + b % 2, q * P:(q + 1) * P], y_all[:, b * TQ + q, :], ident[:, :])
                last.then_inc(s_byt, 1)
            te.wait_ge(s_bytc, B)
            for j in range(NT):
                last = mm(bank[:, 1, j * NE:(j + 1) * NE], yT_all[:, j * P:(j + 1) * P], gate_w[:, :],
                          start=True, stop=True)
            last.then_inc(s_logit, 1)
            te.wait_ge(s_before, 1)
            te.wait_ge(s_setup, 7)
            taken_all = chosen_e[:, :, :].rearrange("p e j -> p (e j)")
            mm(bank[:, 7, 0:NE * NT], strict[:, :], taken_all, start=True, stop=True)
            mm(bank[:, 0, 0:NE * NT], all_ones[:, :], taken_all, start=True, stop=True).then_inc(s_total, 1)

            def shared(b):
                for k in range(SHT):
                    c = slice(k * P, (k + 1) * P)
                    if k >= 2:
                        te.wait_ge(s_actv, SHT * b + k - 1)
                    g = 2 + 2 * (k % 2)
                    yT_b = yT_all[:, ds(b * T, T)]
                    mm(bank[:, g, :], sw1[:, c], yT_b, start=True, stop=True)
                    mm(bank[:, g + 1, :], sw3[:, c], yT_b, start=True, stop=True).then_inc(s_gu, 1)
                te.wait_ge(s_actv, SHT * b + SHT)
                for q in range(TQ):
                    for k in range(SHT):
                        last = mm(bank[:, 6, q * P:(q + 1) * P], act[:, k, q * P:(q + 1) * P],
                                  sw2[:, k, :], start=(k == 0), stop=(k == SHT - 1))
                last.then_inc(s_ye, 1)

            def expert_of(n):
                return te.value_load(owner[0:1, ds(n, 1)], min_val=0, max_val=NE - 1)

            def up(n, m):
                te.wait_ge(s_trc, n + 1)
                te.nop().then_inc(s_apart_te, 1)
                e = expert_of(n)
                for a, w in enumerate((w1, w3)):
                    last = mm(bank[:, 2 + 2 * (m % 2) + a, 0:HID], turned[:, (m - 2) % 4, HT, :],
                              w[:, ds(e, 1), :].rearrange("p a n -> p (a n)"), start=True, stop=True)
                last.then_inc(s_eup, 1)

            def turn(n, m, hidden=True, rows=True):
                if hidden:
                    te.wait_ge(s_eact, n)
                    for k in range(HT):
                        last = te.transpose(bank[:, 6 + m % 2, k * P:(k + 1) * P],
                                            act[:, SHT + (m - 1) % 2, k * P:(k + 1) * P], ident[:, :])
                if rows:
                    x = (m + 2) % 8
                    if x % TQ == 0:
                        te.wait_ge(s_xload[x // TQ], 16 * (load_turn(n, m) + 1))
                    last = te.transpose(bank[:, 6 + m % 2, HT * P:(HT + 1) * P], x_rows[:, x // TQ, x % TQ, :],
                                        ident[:, :])
                last.then_inc(s_tr, 1)

            def down(n, m):
                te.wait_ge(s_trc, n + 4)
                if m % TQ == 0:
                    wait(te, s_erows, group_of(n, m) - 1)
                te.nop().then_inc(s_apart_te, 1)
                e = expert_of(n)
                for k in range(HT):
                    last = mm(bank[:, (m % 8) // TQ, (m % TQ) * P:(m % TQ + 1) * P], turned[:, (m + 1) % 4, k, :],
                              w2[:, ds(e, 1), k, :].rearrange("p a n -> p (a n)"), start=(k == 0), stop=(k == HT - 1))
                last.then_inc(s_edown, 1)

            with te.Fori(0, B // 2) as b:
                shared(b)
            te.wait_ge(s_yec, B // 2)
            te.wait_ge(s_owner, 1)
            cur = {}

            def load_turn(n, m):
                return cur["i"] + (m + 2) // 8

            def group_of(n, m):
                return 2 * cur["i"] + m // TQ

            def tiles(i):
                cur["i"] = i
                for m in range(8):
                    n = 8 * i + m
                    up(n, m)
                    turn(n, m, hidden=not (isinstance(n, int) and n == 0), rows=not (isinstance(n, int) and n + 2 >= XT))
                    if not (isinstance(n, int) and n < 2):
                        down(n - 2, m - 2)

            cur["i"] = 0
            turn(-2, -2, hidden=False)
            turn(-1, -1, hidden=False)
            turns(te, XT // 8, tiles, last=True)
            cur["i"] = XT // 8
            turn(XT, 0, rows=False)
            down(XT - 2, -2)
            down(XT - 1, -1)
            with te.Fori(B // 2, B) as b:
                shared(b)
            phase_end(te, 1)
            if upto < 2:
                return

            te.wait_ge(s_weights1, 16 * len(WEIGHTS1))
            te.wait_ge(s_setup, 12)

            def turn(b, bx, bg, par):
                for e in range(DK):
                    if b is not None:
                        for ahead in ((0, 1) if e == 0 else (e + 1,)):
                            if ahead < DK:
                                broadcast_v(b, par, ahead)
                        broadcast_k(b, par, e)
                        if e >= 2:
                            add_term(b, bg, e - 2)
                        elif bg is not None:
                            add_term(bg, None, DK + e - 2)
                    if bg is not None and e in FINISH:
                        FINISH[e](bg)
                    if bx is not None and e in READY:
                        READY[e](bx, 1 - par)

            def broadcast_v(b, par, e):
                wait(te, s_vbc, DK * b + e - 1)
                for lo in range(2):
                    last = mm(bank[:, 1 + e % 2, :], pick[:, e, :], part1[:, par, 2 + lo, :],
                              start=(lo == 0), stop=(lo == 1))
                last.then_inc(s_vb, 1)

            def broadcast_k(b, par, e):
                wait(te, s_term, DK * b + e - 1)
                for lo in range(2):
                    last = mm(bank[:, 3 + e % 2, :], pick[:, e, :], part1[:, par, lo, :],
                              start=(lo == 0), stop=(lo == 1))
                last.then_inc(s_kb, 1)

            def add_term(b, bg, e):
                te.wait_ge(s_term, DK * b + e + 1)
                if e == 0 and bg is not None:
                    te.wait_ge(s_wkv, bg + 1)
                mm(bank[:, 7, :], ident[:, :], term[:, e % 2, :], start=(e == 0),
                   stop=(e == DK - 1)).then_inc(s_acc, 1)

            def sum_means(b):
                te.wait_ge(s_gm, 2 * b + 1)
                mm(bank[:, 0, 0:1], head_ones[:, :], gn_mv[:, 0:1], start=True, stop=True).then_inc(s_gmr, 1)

            def sum_variances(b):
                te.wait_ge(s_gm, 2 * b + 2)
                mm(bank[:, 0, 2:3], head_ones[:, :], gn_dev[:, :], start=True, stop=True).then_inc(s_gmr, 1)

            def output(b):
                te.wait_ge(s_on, b + 1)
                for q in range(TQ):
                    last = mm(bank[:, 0, q * P:(q + 1) * P], wkv[:, q * P:(q + 1) * P], wout[:, :],
                              start=True, stop=True)
                last.then_inc(s_co, 1)

            def turn_tokens(b, par):
                wait(te, s_sig, 2 * b)
                te.wait_ge(s_cy, b + 1)
                for q in range(TQ):
                    last = te.transpose(bank[:, 6, q * P:(q + 1) * P], y[:, q, :], ident[:, :])
                last.then_inc(s_cyt, 1)

            def project(bk, m):
                te_out = bank[:, bk, :]
                return mm(te_out, mix_w[:, m, :], mixed[:, m, :] if m < 4 else yT[:, :],
                          start=True, stop=True).then_inc(s_proj, 1)

            def project_wk(b, par):
                te.wait_ge(s_mix, 4 * b + 1)
                project(5, 3)
                te.wait_ge(s_mix, 4 * b + 2)
                project(6, 1)

            def project_r(b, par):
                te.wait_ge(s_mix, 4 * b + 3)
                te.wait_ge(s_w, 3 * b + 1)
                project(5, 0)

            def project_v(b, par):
                te.wait_ge(s_mix, 4 * b + 4)
                project(0, 2)

            def project_g(b, par):
                te.wait_ge(s_hi, 3 * b + 2)
                te.wait_ge(s_lo, 2 * b + 1)
                project(6, 4)

            def sum_v(b, par):
                te.wait_ge(s_hi, 3 * b + 3)
                te.wait_ge(s_lo, 2 * b + 2)
                for lo in range(2):
                    last = mm(bank[:, 0, :], head_ones_r[:, :], part1[:, par, 2 + lo, :],
                              start=(lo == 0), stop=(lo == 1))
                last.then_inc(s_vsum, 1)

            FINISH = {3: sum_means, 5: sum_variances, 9: output}
            READY = {3: turn_tokens, 7: project_wk, 10: project_r, 11: project_v, 12: project_g, 14: sum_v}
            turn(None, 0, None, 1)
            turn(0, 1, None, 0)
            with te.Fori(0, B // 2 - 1) as i:
                turn(2 * i + 1, 2 * i + 2, 2 * i, 1)
                turn(2 * i + 2, 2 * i + 3, 2 * i + 1, 0)
            turn(B - 1, None, B - 2, 1)
            for e in (DK - 2, DK - 1):
                add_term(B - 1, None, e)
            for e in FINISH:
                FINISH[e](B - 1)
            phase_end(te, 2)
            if upto < 3:
                return

            te.wait_ge(s_weights2, 16 * len(WEIGHTS2))
            def logits_of(b):
                te.wait_ge(s_dytc, b + 1)
                if b >= 2:
                    te.wait_ge(s_dlc, b - 1)
                mm(bank[0:NE, 2 + b % 2, :], router[:, :], pickedT[:, b % 2, :], start=True, stop=True).then_inc(s_dl, 1)

            for b in range(B):
                te.wait_ge(s_dy, b + 1)
                if b >= 2:
                    te.wait_ge(s_dytc, b - 1)
                for q in range(TQ):
                    last = te.transpose(bank[:, b % 2, q * P:(q + 1) * P], picked[:, b % 2, q, :], ident[:, :])
                last.then_inc(s_dyt, 1)
                if b:
                    logits_of(b - 1)
            logits_of(B - 1)
            phase_end(te, 3)
            te.wait_ge(s_ptop, 1)
            te.transpose(bank[0:1, 4, 0:P], part_top[:, :], ident[:, :]).then_inc(s_ptopt, 1)
            te.wait_ge(s_etop, 1)
            mm(bank[:, 5, 0:1], top_row[:, :, :].rearrange("p e c -> p (e c)"), ones_row[:, 0:1],
               start=True, stop=True).then_inc(s_ebias, 1)
            te.wait_ge(s_pexp, 1)
            mm(bank[:, 6, 0:1], same_e[:, :], part_sum[:, :], start=True, stop=True).then_inc(s_psum, 1)
            with te.Fori(0, 30) as i:
                te.wait_ge(s_cnt, i + 1)
                mm(bank[:, 0, 0:1], same_e[:, :], count[:, :], start=True, stop=True).then_inc(s_tot, 1)
            te.wait_ge(s_cnt, 31)
            mm(bank[:, 0, 1:2], same_e[:, :], count[:, :], start=True, stop=True).then_inc(s_tot, 1)
            te.wait_ge(s_cnt, 32)
            mm(bank[:, 0, 2:3], before[:, :], count[:, :], start=True, stop=True).then_inc(s_tot, 1)
            te.wait_ge(s_cnt, 33)
            mm(bank[:, 0, 3:4], before[:, :], count[:, :], start=True, stop=True).then_inc(s_tot, 1)
            te.wait_ge(s_slots, 1)
            for n in range(2):
                te.transpose(bank[:, 1, n * P:(n + 1) * P], slot[:, n * P:(n + 1) * P], ident[:, :])
                last = te.transpose(bank[:, 1, (2 + n) * P:(3 + n) * P], prob[:, n * P:(n + 1) * P], ident[:, :])
            last.then_inc(s_slotst, 1)
            te.wait_ge(s_zero, 1)
            W = 5 * SH
            lists = bank[:, 2, 0:NE * W]
            mm(lists, zeros[:, 0:P], zeros[:, :], start=True, stop=True)
            te.wait_ge(s_entry, 1)

            def place(c, par):
                te.wait_ge(s_hot, c + 1)
                for n in range(2 * NE):
                    x = n % NE
                    col = (n // NE) * P + x * NC + c
                    mm(bank[:, 2, x * W:(x + 1) * W], onehot[:, par, n, :],
                       entry[:, ds(col, 1), :, :].rearrange("p a k s -> p (a k s)"),
                       start=False, stop=True, skip_group_check=True).then_inc(s_hotc, 1)

            def two_chunks(i):
                for par in range(2):
                    place(2 * i + par, par)

            turns(te, NC // 2, two_chunks)
            phase_end(te, 4)

            def experts(i):
                for m in range(4):
                    n, x = 4 * i + m, m // 2
                    te.wait_ge(s_gather[m % 2], 16 * TQ * (2 * i + x + 1))
                    for q in range(TQ):
                        last = te.transpose(bank[:, m % 2, q * P:(q + 1) * P], picked[:, m % 2, q, :], ident[:, :])
                    last.then_inc(s_xt, 1)
                    if not (isinstance(i, int) and m == 0):
                        down_block(i, m - 1)
                    te.wait_ge(s_xtc, n + 1)
                    te.wait_ge(s_load[x], 32 * (i + 1))
                    for k in range(FT):
                        mm(bank[:, 2 + k, :], f1[:, x, k * P:(k + 1) * P], pickedT[:, m % 2, :],
                           start=True, stop=True).then_inc(s_up, 1)

            def down_block(i, m):
                n = 4 * i + m
                x, expert = (m // 2) % 2, 2 * i + (m // 2)
                te.wait_ge(s_gelu, FT * n + FT)
                wait(te, s_wy, n - 1)
                for q in range(TQ):
                    o = bank[:, 6 + m % 2, q * P:(q + 1) * P]
                    for k in range(FT):
                        mm(o, act[:, FT * (m % 2) + k, q * P:(q + 1) * P], f2[:, x, k, :], start=(k == 0), stop=False)
                    last = mm(o, ones_row[:, 0:P], fb2_row[:, ds(D * expert, D)], start=False, stop=True)
                last.then_inc(s_fo, 1)

            turns(te, NE // 2, experts)
            down_block(NE // 2, -1)
            phase_end(te, 5)


def host_layout(x):
    import numpy as np

    f = np.float32
    c = np.ascontiguousarray
    D, NH, DK, T = 128, 8, 16, 512

    def pad_heads(w):
        o = np.zeros((w.shape[0], 2, 4, 32), f)
        o[..., :DK] = w.reshape(w.shape[0], 2, 4, DK)
        return o.reshape(w.shape[0], 256)

    pos = np.arange(T, dtype=f)[:, None]
    div = np.exp(np.arange(0, DK, 2, dtype=f) * f(-(np.log(10000.0) / DK)))
    ang = pos * div[None, :]
    pe = np.stack([np.sin(ang), np.cos(ang)], axis=-1).reshape(T, DK).astype(f)
    spread = np.zeros((128, 4, 4, 2, 64), f)
    for p in range(4):
        for hh in range(2):
            for d in range(DK):
                src = (2 * p + hh) * DK + d
                spread[src, 0, p, hh, [d, 2 * DK + d]] = 1
                spread[src, 1, p, hh, DK + d] = 1
                spread[src, 2, p, hh, [d, DK + d]] = 1
                spread[src, 3, p, hh, 2 * DK + d] = 1
    ones_rows = np.zeros((2, 64), f)
    ones_rows[:, 3 * DK:3 * DK + 2] = 1
    pick = np.zeros((128, 4), f)
    for j in range(4):
        pick[32 * j + DK, j] = 1
    zero = np.zeros(D, f)
    vec = c(np.stack([x["L0_attn_ln_g"], x["L0_attn_ln_b"], x["L0_attn_bq"], x["L0_attn_bk"],
                      ones_rows.reshape(-1), zero, zero, zero], axis=1))
    head = np.arange(128) // DK
    head_ones = (head[:, None] == head[None, :]).astype(f)
    pick_e = np.zeros((128, DK, 128), f)
    for e in range(DK):
        pick_e[:, e, :] = head_ones * (np.arange(128) % DK == e)[:, None]
    tri = np.tril(np.ones((8, 8), f), -1).reshape(1, 64)
    return {
        "x": c(x["x"].reshape(32, 128).T),
        "emb": c(x["L0_tok_W"].T),
        "tok_b": x["L0_tok_b"],
        "vec": vec,
        "ident": np.eye(128, dtype=f),
        "wq": c(x["L0_attn_wq"].T), "wk": c(x["L0_attn_wk"].T),
        "wv": c(x["L0_attn_wv"].T),
        "wo": c(pad_heads(x["L0_attn_wo"]).T.reshape(2, 128, 128)),
        "bo": x["L0_attn_bo"].reshape(1, D), "bv": x["L0_attn_bv"],
        "pe": c(np.tile(pe.T, (NH, 1))),
        "spread": spread.reshape(128, 4, 512),
        "pick_sum": pick,
        "gate_w": c(x["L0_ffn_gate_w"].T),
        "w1": c(x["L0_ffn_w1"].transpose(0, 2, 1)), "w3": c(x["L0_ffn_w3"].transpose(0, 2, 1)),
        "w2": c(x["L0_ffn_w2"].transpose(0, 2, 1)),
        "sw1": c(x["L0_ffn_sw1"].T), "sw3": c(x["L0_ffn_sw3"].T), "sw2": c(x["L0_ffn_sw2"].T),
        "tri": tri.reshape(64),
        "strict": np.triu(np.ones((128, 128), f), 1),
        "tile_up": np.arange(72, dtype=f).reshape(1, 72),
        "mix_w": c(np.stack([x["L1_attn_" + n].T for n in ("Wr", "Wk", "Wv", "Ww", "Wg")])),
        "wout": c(x["L1_attn_Wout"].T),
        "vec1": c(np.stack([x["L1_attn_" + n].reshape(-1) for n in
                            ("mu_r", "mu_k", "mu_v", "mu_w", "decay_A", "decay_B", "decay_base", "u",
                             "gn_w", "gn_b")], axis=1)),
        "pick": pick_e.reshape(128, 2048),
        "head_ones": head_ones,
        "router": x["L1_ffn_Wr"], "f1": x["L1_ffn_W1"], "f2": x["L1_ffn_W2"],
        "fb1": c(x["L1_ffn_b1"].reshape(32, 128).T), "fb2": x["L1_ffn_b2"].reshape(1, 1024),
        "bits": np.tile((1 << np.arange(29, -1, -1)).astype(np.int32), (128, 1)),
        "tile_no": c(np.tile((2 * np.arange(16)[None, None, :] + np.arange(2)[:, None, None]
                              + np.zeros((2, 8, 16))).reshape(1, 256).astype(f), (128, 1))),
        "count_up": np.tile(np.arange(128, dtype=f), (128, 1)),
        "row_no": np.arange(128, dtype=f).reshape(128, 1),
        "before": c(head_ones * np.triu(np.ones((128, 128), f), 1)),
    }


def kernel(**inputs):
    import numpy as _np
    import concourse.bacc as _bacc
    from concourse import mybir as _mybir
    from concourse.bass_utils import run_bass_kernel_spmd as _run

    nc = _bacc.Bacc("TRN2", target_bir_lowering=False, num_devices=1)
    laid = host_layout({k: _np.asarray(v) for k, v in inputs.items()})
    arrays = {f"in_{k}": v for k, v in laid.items()}
    aps = {k: nc.dram_tensor(f"in_{k}", v.shape, _mybir.dt.from_np(v.dtype), kind="ExternalInput").ap()
           for k, v in laid.items()}
    out = nc.dram_tensor("out", (8, 512, 128), _mybir.dt.float32, kind="ExternalOutput").ap()
    lm_tower(nc, aps, out)
    r = _run(nc, [arrays], core_ids=[0])
    return r.results[0]["out"]
```
